# Optimizing a Trainium2 kernel written in Bass

```python
import numpy as np
import jax
import jax.numpy as jnp

def _softmax(x, axis=-1):
    return jax.nn.softmax(x, axis=axis)

def _gelu(x):
    return jax.nn.gelu(x, approximate=True)

def _silu(x):
    return jax.nn.silu(x)

def _sigmoid(x):
    return jax.nn.sigmoid(x)

def _layernorm(x, axis=-1, eps=1e-05):
    m = jnp.mean(x, axis=axis, keepdims=True)
    v = jnp.var(x, axis=axis, keepdims=True)
    return (x - m) / jnp.sqrt(v + eps)

def _scatter_add(tgt, idx, src, axis=0):
    return tgt.at[idx].add(src)

def _segment_sum(src, seg, n):
    return jax.ops.segment_sum(src, seg, n)
kernel_name = 'mk_gnn_resnorm_d4_gnn_r16_1fafc5'

def setup_inputs(seed: int=0):
    np.random.seed(seed)
    _w = jnp.asarray

    def _rec_inputs():
        import jax
        import jax.numpy as jnp
        _gk = jax.random.key(seed)
        x = -0.0001006 + 1 * jax.random.normal(jax.random.fold_in(_gk, 1), (3125, 96), jnp.float32)
        _s = jax.random.randint(jax.random.fold_in(_gk, 2), (25000,), 0, 3125, jnp.int32)
        _d = jax.random.randint(jax.random.fold_in(_gk, 3), (25000,), 0, 3125, jnp.int32)
        _loop = jnp.arange(3125, dtype=jnp.int32)
        src = jnp.concatenate([_s, _d, _loop])
        dst = jnp.concatenate([_d, _s, _loop])
        _o = jnp.argsort(dst, stable=True)
        src = src[_o]
        dst = dst[_o]
        edge_attr_32 = 0.000196303 + 1.00016 * jax.random.normal(jax.random.fold_in(_gk, 11), (53125, 32), jnp.float32)
        return (x, src, dst, edge_attr_32)
    x, src, dst, edge_attr_32 = _rec_inputs()

    def _L0_gnn_setup():
        import jax, jax.numpy as jnp
        import numpy as np
        N_NODES = 3125
        N_FEAT = 96
        N_EDGES = 50000
        K_HOPS = 2
        key = jax.random.key(seed)
        k1, k2 = jax.random.split(key)
        x = jax.random.normal(k1, (N_NODES, N_FEAT), dtype=jnp.float32)
        edge_index = jax.random.randint(k2, (2, N_EDGES), 0, N_NODES, dtype=jnp.int64)
        return {'x': x, 'edge_index': edge_index}
    _L0_gnn_all = _L0_gnn_setup()
    _L0_gnn_in = {k: v for k, v in _L0_gnn_all.items() if k in ()}
    del _L0_gnn_all

    def _L1_gnn_setup():
        import jax, jax.numpy as jnp
        import numpy as np
        N, E = (3125, 50000)
        DIN = DOUT = 96
        DE = 32

        def _egnn_conv(x, src, dst, edge_attr, W_msg, W_edge, W_root, b):
            msg = x[src] @ W_msg + edge_attr @ W_edge
            agg = jax.ops.segment_max(msg, dst, num_segments=x.shape[0])
            agg = jnp.where(jnp.isneginf(agg), 0.0, agg)
            return agg + x @ W_root + b
        key = jax.random.key(seed)
        ks = jax.random.split(key, 10)
        rn = lambda k, sh, sc: jax.random.normal(k, sh, jnp.float32) * sc
        return {'X': rn(ks[0], (N, DIN), 1.0), 'edge_index': jax.random.randint(ks[1], (2, E), 0, N, jnp.int32), 'edge_attr': rn(ks[2], (E, DE), 1.0), 'W1_msg': rn(ks[3], (DIN, DOUT), DIN ** (-0.5)), 'W1_edge': rn(ks[4], (DE, DOUT), DE ** (-0.5)), 'W1_root': rn(ks[5], (DIN, DOUT), DIN ** (-0.5)), 'b1': jnp.zeros((DOUT,), jnp.float32), 'W2_msg': rn(ks[6], (DOUT, DOUT), DOUT ** (-0.5)), 'W2_edge': rn(ks[7], (DE, DOUT), DE ** (-0.5)), 'W2_root': rn(ks[8], (DOUT, DOUT), DOUT ** (-0.5)), 'b2': jnp.zeros((DOUT,), jnp.float32)}
    _L1_gnn_all = _L1_gnn_setup()
    _L1_gnn_in = {k: v for k, v in _L1_gnn_all.items() if k in ('W1_msg', 'W1_edge', 'W1_root', 'b1', 'W2_msg', 'W2_edge', 'W2_root', 'b2')}
    del _L1_gnn_all

    def _L2_gnn_setup():
        import jax, jax.numpy as jnp
        import numpy as np
        K = 16
        ALPHA = 0.1
        key = jax.random.key(seed)
        k1, k2 = jax.random.split(key)
        N, E, D = (3125, 50000, 96)
        x = jax.random.normal(k1, (N, D), dtype=jnp.float32)
        edge_index = jax.random.randint(k2, (2, E), 0, N, dtype=jnp.int64)
        return {'x': x, 'edge_index': edge_index}
    _L2_gnn_all = _L2_gnn_setup()
    _L2_gnn_in = {k: v for k, v in _L2_gnn_all.items() if k in ()}
    del _L2_gnn_all

    def _L3_gnn_setup():
        import jax, jax.numpy as jnp
        import numpy as np
        from jax.ops import segment_sum
        N_NODES = 3125
        N_EDGES = 50000
        D_IN = 96
        D_OUT = 96
        EPS = 1e-05

        def _gcn_conv(x, row, col, n, W, b):
            ones = jnp.ones(row.shape[0], dtype=x.dtype)
            deg = segment_sum(ones, col, num_segments=n)
            dinv = jnp.where(deg > 0, jax.lax.rsqrt(deg), 0.0)
            norm = dinv[row] * dinv[col]
            xw = x @ W
            msg = xw[row] * norm[:, None]
            return segment_sum(msg, col, num_segments=n) + b
        key = jax.random.key(seed)
        ks = jax.random.split(key, 9)
        return {'x': jax.random.normal(ks[0], (N_NODES, D_IN), dtype=jnp.float32), 'edge_index': jax.random.randint(ks[1], (2, N_EDGES), 0, N_NODES, dtype=jnp.int64), 'W1': jax.random.normal(ks[2], (D_IN, D_IN), dtype=jnp.float32) / np.sqrt(D_IN), 'b1': jax.random.normal(ks[3], (D_IN,), dtype=jnp.float32) * 0.1, 'gn_weight': 1.0 + 0.1 * jax.random.normal(ks[4], (D_IN,), dtype=jnp.float32), 'gn_bias': 0.1 * jax.random.normal(ks[5], (D_IN,), dtype=jnp.float32), 'gn_mean_scale': 1.0 + 0.1 * jax.random.normal(ks[6], (D_IN,), dtype=jnp.float32), 'W2': jax.random.normal(ks[7], (D_IN, D_OUT), dtype=jnp.float32) / np.sqrt(D_IN), 'b2': jax.random.normal(ks[8], (D_OUT,), dtype=jnp.float32) * 0.1}
    _L3_gnn_all = _L3_gnn_setup()
    _L3_gnn_in = {k: v for k, v in _L3_gnn_all.items() if k in ('W1', 'b1', 'gn_weight', 'gn_bias', 'gn_mean_scale', 'W2', 'b2')}
    del _L3_gnn_all
    return {'x': x, 'src': src, 'dst': dst, 'edge_attr_32': edge_attr_32, 'L1_gnn_W1_msg': _L1_gnn_in['W1_msg'], 'L1_gnn_W1_edge': _L1_gnn_in['W1_edge'], 'L1_gnn_W1_root': _L1_gnn_in['W1_root'], 'L1_gnn_b1': _L1_gnn_in['b1'], 'L1_gnn_W2_msg': _L1_gnn_in['W2_msg'], 'L1_gnn_W2_edge': _L1_gnn_in['W2_edge'], 'L1_gnn_W2_root': _L1_gnn_in['W2_root'], 'L1_gnn_b2': _L1_gnn_in['b2'], 'L3_gnn_W1': _L3_gnn_in['W1'], 'L3_gnn_b1': _L3_gnn_in['b1'], 'L3_gnn_gn_weight': _L3_gnn_in['gn_weight'], 'L3_gnn_gn_bias': _L3_gnn_in['gn_bias'], 'L3_gnn_gn_mean_scale': _L3_gnn_in['gn_mean_scale'], 'L3_gnn_W2': _L3_gnn_in['W2'], 'L3_gnn_b2': _L3_gnn_in['b2']}

def reference(x, src, dst, edge_attr_32, L1_gnn_W1_msg, L1_gnn_W1_edge, L1_gnn_W1_root, L1_gnn_b1, L1_gnn_W2_msg, L1_gnn_W2_edge, L1_gnn_W2_root, L1_gnn_b2, L3_gnn_W1, L3_gnn_b1, L3_gnn_gn_weight, L3_gnn_gn_bias, L3_gnn_gn_mean_scale, L3_gnn_W2, L3_gnn_b2):
    import jax
    import jax.numpy as jnp

    def _L0_gnn_ref(x, edge_index):
        import jax, jax.numpy as jnp
        import numpy as np
        N_NODES = 3125
        N_FEAT = 96
        N_EDGES = 50000
        K_HOPS = 2
        N = x.shape[0]
        loops = jnp.arange(N, dtype=edge_index.dtype)
        src = jnp.concatenate([edge_index[0], loops])
        dst = jnp.concatenate([edge_index[1], loops])
        ew = jnp.ones(src.shape[0], dtype=x.dtype)
        deg = jax.ops.segment_sum(ew, dst, num_segments=N)
        deg_inv_sqrt = jnp.where(deg > 0, jax.lax.rsqrt(deg), jnp.zeros_like(deg))
        norm = deg_inv_sqrt[src] * ew * deg_inv_sqrt[dst]

        def hop(h):
            return jax.ops.segment_sum(norm[:, None] * h[src], dst, num_segments=N)
        h = x
        for _ in range(K_HOPS):
            h = hop(h)
        return h

    def _L1_gnn_ref(X, edge_index, edge_attr, W1_msg, W1_edge, W1_root, b1, W2_msg, W2_edge, W2_root, b2):
        import jax, jax.numpy as jnp
        import numpy as np
        N, E = (3125, 50000)
        DIN = DOUT = 96
        DE = 32

        def _egnn_conv(x, src, dst, edge_attr, W_msg, W_edge, W_root, b):
            msg = x[src] @ W_msg + edge_attr @ W_edge
            agg = jax.ops.segment_max(msg, dst, num_segments=x.shape[0])
            agg = jnp.where(jnp.isneginf(agg), 0.0, agg)
            return agg + x @ W_root + b
        src, dst = (edge_index[0], edge_index[1])
        c1 = jax.nn.leaky_relu(_egnn_conv(X, src, dst, edge_attr, W1_msg, W1_edge, W1_root, b1))
        c2 = jax.nn.leaky_relu(_egnn_conv(c1, src, dst, edge_attr, W2_msg, W2_edge, W2_root, b2))
        return c2

    def _L2_gnn_ref(x, edge_index):
        import jax, jax.numpy as jnp
        import numpy as np
        K = 16
        ALPHA = 0.1
        N = x.shape[0]
        loop = jnp.arange(N, dtype=edge_index.dtype)
        row = jnp.concatenate([edge_index[0], loop])
        col = jnp.concatenate([edge_index[1], loop])
        deg = jax.ops.segment_sum(jnp.ones_like(col, dtype=x.dtype), col, num_segments=N)
        deg_inv_sqrt = jnp.where(deg > 0, jax.lax.rsqrt(jnp.maximum(deg, 1e-30)), 0.0)
        norm = (deg_inv_sqrt[row] * deg_inv_sqrt[col])[:, None]
        h = x
        for _ in range(K):
            h_neighbors = jax.ops.segment_sum(norm * h[row], col, num_segments=N)
            h = (1.0 - ALPHA) * h_neighbors + ALPHA * x
        return h

    def _L3_gnn_ref(x, edge_index, W1, b1, gn_weight, gn_bias, gn_mean_scale, W2, b2):
        import jax, jax.numpy as jnp
        import numpy as np
        from jax.ops import segment_sum
        N_NODES = 3125
        N_EDGES = 50000
        D_IN = 96
        D_OUT = 96
        EPS = 1e-05

        def _gcn_conv(x, row, col, n, W, b):
            ones = jnp.ones(row.shape[0], dtype=x.dtype)
            deg = segment_sum(ones, col, num_segments=n)
            dinv = jnp.where(deg > 0, jax.lax.rsqrt(deg), 0.0)
            norm = dinv[row] * dinv[col]
            xw = x @ W
            msg = xw[row] * norm[:, None]
            return segment_sum(msg, col, num_segments=n) + b
        n = x.shape[0]
        loops = jnp.arange(n, dtype=edge_index.dtype)
        row = jnp.concatenate([edge_index[0], loops])
        col = jnp.concatenate([edge_index[1], loops])
        h = _gcn_conv(x, row, col, n, W1, b1)
        mean = jnp.mean(h, axis=0)
        hc = h - gn_mean_scale * mean
        var = jnp.mean(hc * hc, axis=0)
        h = gn_weight * hc * jax.lax.rsqrt(var + EPS) + gn_bias
        h = jax.nn.relu(h)
        return _gcn_conv(h, row, col, n, W2, b2)
    edge_index = jnp.stack([src, dst])
    x = _layernorm(x + _L0_gnn_ref(x, edge_index), axis=-1)
    x = _layernorm(x + _L1_gnn_ref(x, edge_index, edge_attr_32, L1_gnn_W1_msg, L1_gnn_W1_edge, L1_gnn_W1_root, L1_gnn_b1, L1_gnn_W2_msg, L1_gnn_W2_edge, L1_gnn_W2_root, L1_gnn_b2), axis=-1)
    x = _layernorm(x + _L2_gnn_ref(x, edge_index), axis=-1)
    x = _layernorm(x + _L3_gnn_ref(x, edge_index, L3_gnn_W1, L3_gnn_b1, L3_gnn_gn_weight, L3_gnn_gn_bias, L3_gnn_gn_mean_scale, L3_gnn_W2, L3_gnn_b2), axis=-1)
    return x

_drawn_inputs = setup_inputs


def setup_inputs(seed=0):
    import zlib

    import numpy as np

    out = dict(_drawn_inputs(seed))
    spreads = {'L1_gnn_b1': (0.0, 0.1), 'L1_gnn_b2': (0.0, 0.267)}
    factors = {}
    for name, (base, spread) in spreads.items():
        noise = np.random.default_rng([zlib.crc32(name.encode()), seed]).standard_normal(out[name].shape)
        drawn = base * np.exp(spread * noise) if base else spread * noise
        out[name] = jnp.asarray(drawn.astype(out[name].dtype))
    for name, factor in factors.items():
        out[name] = (out[name] * factor).astype(out[name].dtype)
    return out
```

```python
import concourse.bass as bass
from concourse import mybir
from contextlib import ExitStack

F32 = mybir.dt.float32
F16 = mybir.dt.float16
BF16 = mybir.dt.bfloat16
I32 = mybir.dt.int32
ALU = mybir.AluOpType
ACT = mybir.ActivationFunctionType
X_AXIS = mybir.AxisListType.X

N, F, DE, E = 3125, 96, 32, 53125
P = 125
T = N // P
C = E // P
LO = 2048.0
NEG = -3.0e38
MAGIC = 1.5 * 2.0 ** 23
K = 128
WK = -(-E // (T * K)) + 1
WIN = WK * K
ATW = N + 3
BLK = 4
NBANK = -(-T // BLK)
TAIL = 3
RING = 6
BANK = 512
G = 5
GE = G * P
HB = 5
EPS = 1e-5


class Chain:

    def __init__(self, eng, sem):
        self.eng, self.sem, self.n = eng, sem, 0

    def __call__(self, ins):
        self.n += 1
        ins.then_inc(self.sem, 1)
        self.eng.wait_ge(self.sem, self.n)


def build(nc, x, src, dst, src_cols, ea_t, w, out):
    top = ExitStack()
    with top:
        def keep(name, shape, dt):
            return top.enter_context(nc.sbuf_tensor(name, shape, dt))

        def sem(name):
            return top.enter_context(nc.semaphore(name))

        at = keep("counts", [P, T, ATW], F16)
        ident = keep("ident", [128, 128], F32)
        dinv = keep("dinv", [P, T], F32)
        dsqrt = keep("dsqrt", [P, T], F32)
        has_in = keep("has_in", [P, T], F32)
        end_idx = keep("end_idx", [P, T], I32)
        start_f = keep("start_f", [1, T], F32)

        ev_d = nc.dram_tensor("edge_values", (3, E + WIN), F32).ap()
        mask_d = nc.dram_tensor("segment_mask", (1, E), BF16).ap()
        y_d = nc.dram_tensor("messages", (N, F), F32).ap()
        x_d = nc.dram_tensor("x_parked", (N, F), F32).ap()
        root_d = nc.dram_tensor("root_parked", (N, F), F32).ap()
        scan_d = nc.dram_tensor("running_max", (E, F), F32).ap()
        ctx = dict(nc=nc, sem=sem, at=at, ident=ident, dinv=dinv, dsqrt=dsqrt, has_in=has_in,
                   end_idx=end_idx, start_f=start_f, ev_d=ev_d, mask_d=mask_d, y_d=y_d, x_d=x_d,
                   root_d=root_d, scan_d=scan_d, w=w)
        build_counts(ctx, src, dst)
        degrees(ctx)
        with ExitStack() as st:
            xs = st.enter_context(nc.sbuf_tensor("x_state", [P, T, F], F32))
            load_nodes(ctx, "x0", xs, x)
            with ExitStack() as s2:
                hs = hop_state(ctx, s2, "l0")
                hop_prepare(ctx, "l0p", hs, xs, 1.0, 0.0)
                hops(ctx, "l0h", hs, 1, True)
                hop_result(ctx, "l0r", hs, hs["uf"], None)
                layer_norm(ctx, "l0n", xs, hs["uf"], hs["xa"])
            with ExitStack() as s2:
                y1 = s2.enter_context(nc.sbuf_tensor("l1_y", [P, T, F], F32))
                node_product(ctx, "c1w", xs, y1, "W1_msg", "W1_root", "b1")
            store_nodes(ctx, "parkx", xs, x_d)
        edge_conv(ctx, "c1", src_cols, ea_t, "W1_edge")
        with ExitStack() as st:
            c1 = st.enter_context(nc.sbuf_tensor("c1", [P, T, F], F32))
            conv_result(ctx, "c1r", c1)
            y2 = st.enter_context(nc.sbuf_tensor("l2_y", [P, T, F], F32))
            node_product(ctx, "c2w", c1, y2, "W2_msg", "W2_root", "b2")
        edge_conv(ctx, "c2", src_cols, ea_t, "W2_edge")
        with ExitStack() as st:
            xs = st.enter_context(nc.sbuf_tensor("x_state2", [P, T, F], F32))
            with ExitStack() as s2:
                c2 = s2.enter_context(nc.sbuf_tensor("c2", [P, T, F], F32))
                sc = s2.enter_context(nc.sbuf_tensor("c2s", [P, T, F], F32))
                conv_result(ctx, "c2r", c2)
                load_nodes(ctx, "x1", xs, x_d)
                layer_norm(ctx, "l1n", xs, c2, sc)
            hs = hop_state(ctx, st, "l2")
            hop_prepare(ctx, "l2p", hs, xs, 0.9, 0.1)
            hops(ctx, "l2h", hs, 8, True)
            hop_result(ctx, "l2r", hs, hs["uf"], None)
            layer_norm(ctx, "l2n", xs, hs["uf"], hs["xa"])
            h = hs["uf"]
            node_product(ctx, "g1w", xs, h, "g_W1", None, None)
            hop_prepare(ctx, "g1p", hs, h, 1.0, 0.0)
            hops(ctx, "g1h", hs, 1, False)
            hop_result(ctx, "g1r", hs, h, "g_b1")
            graph_norm(ctx, "gn", h, hs["xa"])
            node_product(ctx, "g2w", h, h, "g_W2", None, None)
            hop_prepare(ctx, "g2p", hs, h, 1.0, 0.0)
            hops(ctx, "g2h", hs, 1, False)
            hop_result(ctx, "g2r", hs, h, "g_b2")
            layer_norm(ctx, "l3n", xs, h, hs["xa"])
            store_nodes(ctx, "out", xs, out)


def bc(ap, n):
    return ap.unsqueeze(2).to_broadcast([ap.shape[0], ap.shape[1], n])


def node_view(dram):
    return dram.rearrange("(t p) f -> p t f", p=P)


def load_nodes(c, tag, sb, dram):
    s = c["sem"](f"{tag}_ld")
    with c["nc"].Block() as block:
        @block.sync
        def _(sp):
            sp.dma_start(sb[:, :, :], node_view(dram)).then_inc(s, 16)
            sp.wait_ge(s, 16)


def store_nodes(c, tag, sb, dram):
    s = c["sem"](f"{tag}_st")
    with c["nc"].Block() as block:
        @block.sync
        def _(sp):
            sp.dma_start(node_view(dram), sb[:, :, :]).then_inc(s, 16)
            sp.wait_ge(s, 16)



def build_counts(c, src, dst):
    nc, sem, at = c["nc"], c["sem"], c["at"]
    with ExitStack() as st:
        iota = st.enter_context(nc.sbuf_tensor("iota", [K, 2048], F16))
        keys = st.enter_context(nc.sbuf_tensor("keys", [K, T, 3, WK], F32))
        with ExitStack() as s1:
            edge_keys(c, s1, src, dst, iota, keys)
        with ExitStack() as s1:
            table_rounds(c, s1, iota, keys)


def edge_keys(c, st, src, dst, iota, keys):
    nc, sem, ident = c["nc"], c["sem"], c["ident"]

    def sb(name, shape, dt):
        return st.enter_context(nc.sbuf_tensor(name, shape, dt))

    di, si, pv = sb("di", [P, C], I32), sb("si", [P, C], I32), sb("pv", [P, 1], I32)
    ev = sb("ev", [P, 3, C], F32)
    tmp, srcf, pvf = sb("tmp", [P, C], F32), sb("srcf", [P, C], F32), sb("pvf", [P, 1], F32)
    mask = sb("mask", [P, C], BF16)
    pidx, base = sb("pidx", [K, 1], F32), sb("base", [K, T], F32)
    part, ones = sb("part", [P, T], F32), sb("ones", [P, 1], F32)
    pad = sb("pad", [K, 3, WK], F32)
    start_i = sb("start_i", [1, T], I32)
    win = sb("win", [K, T, 3, WK], F32)
    inside = sb("inside", [K, T, WK], F32)
    off = sb("off", [K, T, WK], F32)
    ps = st.enter_context(nc.psum_tensor("sum_ps", [128, BANK], F32))
    s_edge, s_prev, s_iota, s_ch, s_ones = sem("k_edge"), sem("k_prev"), sem("k_iota"), sem("k_chain"), sem("k_ones")
    s_prep, s_below, s_sum, s_start = sem("k_prep"), sem("k_below"), sem("k_sum"), sem("k_start")
    s_ev, s_win, s_mask = sem("k_ev"), sem("k_win"), sem("k_mask")
    dst_v, src_v = (a.rearrange("(p c) -> p c", p=P) for a in (dst, src))

    with nc.Block() as block:
        @block.sync
        def _(sp):
            sp.dma_start(di[:, :], dst_v).then_inc(s_edge, 16)
            sp.dma_start(si[:, :], src_v).then_inc(s_edge, 16)
            sp.wait_ge(s_prep, 1)
            sp.dma_start(c["ev_d"][:, 0:E].rearrange("a (p c) -> p a c", p=P), ev[:, :, :]).then_inc(s_ev, 16)
            sp.dma_start(c["ev_d"][:, E:E + WIN].rearrange("a (p k) -> p a k", p=K), pad[:, :, :]).then_inc(s_ev, 16)
            sp.dma_start(c["mask_d"].rearrange("o (p c) -> (o p) c", p=P), mask[:, :]).then_inc(s_mask, 16)
            sp.wait_ge(s_start, 1)
            sp.wait_ge(s_ev, 32)
            with sp.Fori(0, T) as t:
                first = sp.value_load(start_i[0:1, bass.ds(t, 1)], min_val=0, max_val=E)
                sp.dma_start(win[:, bass.ds(t, 1), :, :].rearrange("p o a k -> p (o a) k"),
                             c["ev_d"][:, bass.ds(first, WIN)].rearrange("a (p k) -> p a k", p=K)).then_inc(s_win, 16)
            sp.wait_ge(s_mask, 16)

        @block.scalar
        def _(act):
            act.wait_ge(s_iota, 4)
            with nc.allow_non_contiguous_dma(reason="the last dst of each partition, single values"):
                act.dma_start(pv[1:P, 0:1], dst_v[0:P - 1, C - 1:C]).then_inc(s_prev, 16)
            act.wait_ge(s_prev, 16)

        @block.gpsimd
        def _(pool):
            pool.memset(pv[:, :], -1).then_inc(s_iota, 1)
            pool.iota(iota[:, :], pattern=[[1, 2048]], base=0, channel_multiplier=0,
                      allow_small_or_imprecise_dtypes=True).then_inc(s_iota, 1)
            pool.iota(pidx[:, :], pattern=[[0, 1]], base=0, channel_multiplier=1,
                      allow_small_or_imprecise_dtypes=True).then_inc(s_iota, 1)
            pool.iota(base[:, :], pattern=[[P, T]], base=0, channel_multiplier=0,
                      allow_small_or_imprecise_dtypes=True).then_inc(s_iota, 1)

        @block.vector
        def _(v):
            ch = Chain(v, s_ch)
            v.memset(ones[:, :], 1.0).then_inc(s_ones, 1)
            v.memset(pad[:, :, :], -1.0)
            v.memset(c["at"][:, :, N:ATW], 0.0)
            v.wait_ge(s_iota, 4)
            v.tensor_scalar(ident[:, :], iota[:, 0:128], pidx[:, :], None, ALU.is_equal)
            v.wait_ge(s_edge, 32)
            v.wait_ge(s_prev, 16)
            v.tensor_copy(pvf[:, :], pv[:, :])
            v.tensor_copy(srcf[:, :], si[:, :])
            ch(v.tensor_copy(ev[:, 2, :], di[:, :]))
            ch(v.tensor_scalar(tmp[:, :], srcf[:, :], float(P // 2), 1.0 / P, ALU.subtract, ALU.mult))
            ch(v.tensor_scalar(tmp[:, :], tmp[:, :], MAGIC, MAGIC, ALU.add, ALU.subtract))
            ch(v.scalar_tensor_tensor(ev[:, 1, :], tmp[:, :], -float(P), srcf[:, :], ALU.mult, ALU.add))
            ch(v.scalar_tensor_tensor(ev[:, 0, :], tmp[:, :], float(P), ev[:, 2, :], ALU.mult, ALU.add))
            v.tensor_tensor(srcf[:, 1:C], ev[:, 2, 1:C], ev[:, 2, 0:C - 1], ALU.not_equal)
            ch(v.tensor_tensor(srcf[:, 0:1], ev[:, 2, 0:1], pvf[:, :], ALU.not_equal))
            v.tensor_scalar(mask[:, :], srcf[:, :], NEG, None, ALU.mult).then_inc(s_prep, 1)
            with v.Fori(0, T) as t:
                v.tensor_scalar(tmp[:, :], ev[:, 2, :], base[0:P, bass.ds(t, 1)], None, ALU.is_lt, ALU.add,
                                accum_out=part[:, bass.ds(t, 1)]).then_inc(s_below, 1)
                v.wait_ge(s_below, t + 1)
            v.wait_ge(s_sum, 1)
            v.tensor_copy(c["start_f"][:, :], ps[0:1, 0:T])
            v.tensor_copy(start_i[:, :], ps[0:1, 0:T]).then_inc(s_start, 1)
            v.wait_ge(s_win, 16 * T)
            q, low, to = (win[:, :, a, :] for a in range(3))
            tile_base = bc(base[:, :], WK)
            ch(v.tensor_tensor(off[:, :, :], to, tile_base, ALU.subtract))
            v.tensor_copy(keys[:, :, 2, :], low)
            v.tensor_scalar(inside[:, :, :], off[:, :, :], float(P), None, ALU.is_lt)
            ch(v.tensor_scalar(off[:, :, :], off[:, :, :], 0.0, None, ALU.is_ge))
            v.tensor_tensor(inside[:, :, :], inside[:, :, :], off[:, :, :], ALU.mult)
            ch(v.tensor_tensor(q, q, tile_base, ALU.subtract))
            ch(v.scalar_tensor_tensor(off[:, :, :], q, 1.0, inside[:, :, :], ALU.add, ALU.mult))
            v.tensor_scalar(keys[:, :, 0, :], off[:, :, :], 1.0, None, ALU.subtract)
            v.tensor_scalar(keys[:, :, 1, :], off[:, :, :], 2049.0, None, ALU.subtract)

        @block.tensor
        def _(pe):
            pe.wait_ge(s_ones, 1)
            pe.wait_ge(s_below, T)
            pe.matmul(ps[0:1, 0:T], ones[:, :], part[:, :], start=True, stop=True).then_inc(s_sum, 1)


def table_rounds(c, st, iota, keys):
    nc, sem, at = c["nc"], c["sem"], c["at"]
    hot = st.enter_context(nc.sbuf_tensor("hot", [K, RING, N + 1], F16))
    low = st.enter_context(nc.sbuf_tensor("low_hot", [K, RING, 128], F16))
    kt = st.enter_context(nc.sbuf_tensor("tile_keys", [K, 3, WK], F32))
    ps = st.enter_context(nc.psum_tensor("count_ps", [128, NBANK, BANK], F32))
    s_key, s_hot, s_used, s_bank, s_flush = (sem(f"t_{n}") for n in ("key", "hot", "used", "bank", "flush"))
    body = WK - TAIL
    USED = WK - 1
    rest = N + 1 - 2048

    def cols(b):
        return (min(BLK, T - b * BLK)) * P

    with nc.Block() as block:
        @block.vector
        def _(v):
            with v.Fori(0, T) as t:
                v.wait_ge(s_hot, t * WK + 1)
                v.tensor_copy(kt[:, :, :], keys[:, bass.ds(t, 1), :, :].rearrange("p o a k -> p (o a) k")).then_inc(s_key, 1)
                v.wait_ge(s_key, t + 1)
                for k in range(WK):
                    r = k % RING
                    if k == RING - 1:
                        v.wait_ge(s_bank, NBANK * t + NBANK)
                    elif k < RING:
                        v.wait_ge(s_used, USED * t + WK - RING + k + 1)
                    else:
                        v.wait_ge(s_used, USED * t + USED + k - RING + 1)
                    v.tensor_scalar(low[:, r, :], iota[:, 0:128], kt[:, 2, k:k + 1], None, ALU.is_equal)
                    v.tensor_scalar(hot[:, r, 0:2048], iota[:, :], kt[:, 0, k:k + 1], None, ALU.is_equal)
                    v.tensor_scalar(hot[:, r, 2048:N + 1], iota[:, 0:rest], kt[:, 1, k:k + 1], None,
                                    ALU.is_equal).then_inc(s_hot, 1)

        @block.tensor
        def _(pe):
            def product(k, b):
                return pe.matmul(ps[:, b, 0:cols(b)], low[:, k % RING, :],
                                 hot[:, k % RING, b * BLK * P:b * BLK * P + cols(b)],
                                 start=(k == 0), stop=(k == WK - 1))
            with pe.Fori(0, T) as t:
                for k in range(body):
                    pe.wait_ge(s_hot, WK * t + k + 2)
                    for b in range(NBANK):
                        if k == 0:
                            pe.wait_ge(s_flush, NBANK * t + b + 1)
                        last = product(k, b)
                    last.then_inc(s_used, 1)
                pe.wait_ge(s_hot, WK * t + WK + 1)
                for b in range(NBANK):
                    for k in range(body, WK):
                        last = product(k, b)
                        if k == WK - 1:
                            last.then_inc(s_bank, 1)
                        elif b == NBANK - 1:
                            last.then_inc(s_used, 1)

        @block.scalar
        def _(act):
            with act.Fori(0, T) as t:
                for b in range(NBANK):
                    act.wait_ge(s_bank, NBANK * t + NBANK + b + 1)
                    n = cols(b) // P
                    act.copy(at[:, b * BLK:b * BLK + n, bass.ds(t * P, P)],
                             ps[0:P, b, 0:cols(b)].rearrange("p (h d) -> p h d", d=P)).then_inc(s_flush, 1)

        @block.gpsimd
        def _(pool):
            pool.sem_inc(s_hot, 1)
            pool.sem_inc(s_used, USED)
            pool.sem_inc(s_bank, NBANK)
            pool.sem_inc(s_flush, NBANK)


def degrees(c):
    nc, sem, at, ident = c["nc"], c["sem"], c["at"], c["ident"]
    with ExitStack() as st:
        def sb(name, shape, dt):
            return st.enter_context(nc.sbuf_tensor(name, shape, dt))
        ones = sb("deg_ones", [P, 2], F16)
        tri, pidx, fidx = sb("tri", [P, P], F32), sb("d_pidx", [P, 1], F32), sb("d_fidx", [P, P], F32)
        one_row = sb("one_row", [1, P], F32)
        deg, loops, y, e, root = (sb(f"d_{n}", [P, T], F32) for n in ("deg", "loops", "y", "e", "root"))
        ps = st.enter_context(nc.psum_tensor("deg_ps", [128, BANK], F32))
        ps2 = st.enter_context(nc.psum_tensor("end_ps", [128, BANK], F32))
        s_one, s_deg, s_ch, s_end, s_iota, s_root = (sem(f"d_{n}") for n in ("one", "deg", "chain", "end", "iota", "root"))
        s_degc, s_sq = sem("d_degc"), sem("d_sq")
        with nc.Block() as block:
            @block.gpsimd
            def _(pool):
                pool.iota(pidx[:, :], pattern=[[0, 1]], base=0, channel_multiplier=1,
                          allow_small_or_imprecise_dtypes=True).then_inc(s_iota, 1)
                pool.iota(fidx[:, :], pattern=[[1, P]], base=0, channel_multiplier=0,
                          allow_small_or_imprecise_dtypes=True).then_inc(s_iota, 1)

            @block.tensor
            def _(pe):
                pe.wait_ge(s_one, 1)
                for t in range(T):
                    for k in range(T):
                        last = pe.matmul(ps[:, t:t + 1], at[:, k, t * P:t * P + 128], ones[:, 0:1],
                                         start=(k == 0), stop=(k == T - 1))
                last.then_inc(s_deg, 1)
                pe.wait_ge(s_degc, 1)
                pe.matmul(ps2[0:P, 0:T], tri[:, :], deg[:, :], start=True, stop=False)
                pe.matmul(ps2[0:P, 0:T], one_row[:, :], c["start_f"][:, :], start=False, stop=True).then_inc(s_end, 1)

            @block.scalar
            def _(act):
                act.wait_ge(s_sq, 1)
                act.activation(root[:, :], loops[:, :], ACT.Sqrt).then_inc(s_root, 1)

            @block.vector
            def _(v):
                ch = Chain(v, s_ch)
                v.memset(ones[:, :], 1.0).then_inc(s_one, 1)
                v.memset(one_row[:, :], 1.0)
                v.wait_ge(s_iota, 2)
                v.tensor_scalar(tri[:, :], fidx[:, :], pidx[:, :], None, ALU.is_ge)
                v.wait_ge(s_deg, 1)
                ch(v.tensor_copy(deg[:, :], ps[0:P, 0:T]))
                v.sem_inc(s_degc, 1)
                v.tensor_scalar(c["has_in"][:, :], deg[:, :], 1.0, None, ALU.min)
                v.tensor_scalar(loops[:, :], deg[:, :], 1.0, None, ALU.add).then_inc(s_sq, 1)
                v.wait_ge(s_sq, 1)
                flat = at[:, :, :].rearrange("p t d -> p (t d)")
                for k in range(T):
                    a = flat[:, k * (ATW + P):k * (ATW + P) + P]
                    v.tensor_tensor(a, a, ident[0:P, 0:P], ALU.add)
                v.wait_ge(s_root, 1)
                ch(v.reciprocal(y[:, :], root[:, :]))
                ch(v.tensor_tensor(e[:, :], y[:, :], y[:, :], ALU.mult))
                ch(v.tensor_tensor(e[:, :], e[:, :], loops[:, :], ALU.mult))
                ch(v.tensor_scalar(e[:, :], e[:, :], -0.5, 1.5, ALU.mult, ALU.add))
                ch(v.tensor_tensor(c["dinv"][:, :], y[:, :], e[:, :], ALU.mult))
                v.scalar_tensor_tensor(c["dsqrt"][:, :], loops[:, :], 1.0 / LO, c["dinv"][:, :], ALU.mult, ALU.mult)
                v.wait_ge(s_end, 1)
                ch(v.tensor_scalar(e[:, :], ps2[0:P, 0:T], 1.0, 0.0, ALU.subtract, ALU.max))
                v.tensor_copy(c["end_idx"][:, :], e[:, :])


def hop_state(c, st, tag):
    nc = c["nc"]

    def sb(name, shape, dt):
        return st.enter_context(nc.sbuf_tensor(f"{tag}_{name}", shape, dt))

    return dict(u=[sb("u0", [P, T, 2 * F], F16), sb("u1", [P, T, 2 * F], F16)], uf=sb("uf", [P, T, F], F32),
                xa=sb("xa", [P, T, F], F32), clo=sb("clo", [P, HB, F], F32),
                cf=sb("cf", [P, T], F32), cl=sb("cl", [P, T], F32))


def hop_prepare(c, tag, h, xs, keep, teleport):
    nc, sem, dinv = c["nc"], c["sem"], c["dinv"]
    s_ch, s_hi, s_uf = sem(f"{tag}_ch"), sem(f"{tag}_hi"), sem(f"{tag}_uf")
    uf, xa, u = h["uf"], h["xa"], h["u"][0]
    with nc.Block() as block:
        @block.vector
        def _(v):
            ch = Chain(v, s_ch)
            ch(v.tensor_tensor(uf[:, :, :], xs[:, :, :], bc(dinv[:, :], F), ALU.mult))
            ch(v.tensor_scalar(uf[:, :, :], uf[:, :, :], LO, None, ALU.mult))
            v.sem_inc(s_uf, 1)
            v.tensor_scalar(xa[:, :, :], uf[:, :, :], teleport, None, ALU.mult)
            ch(v.scalar_tensor_tensor(h["cf"][:, :], dinv[:, :], LO * keep, dinv[:, :], ALU.mult, ALU.mult))
            v.tensor_scalar(h["cl"][:, :], h["cf"][:, :], 1.0 / LO, None, ALU.mult)
            v.wait_ge(s_hi, 1)
            v.scalar_tensor_tensor(u[:, :, F:2 * F], u[:, :, 0:F], -LO, uf[:, :, :], ALU.mult, ALU.add)

        @block.scalar
        def _(act):
            act.wait_ge(s_uf, 1)
            act.activation(u[:, :, 0:F], uf[:, :, :], ACT.Copy, scale=1.0 / LO).then_inc(s_hi, 1)


def hops(c, tag, h, pairs, two):
    nc, sem, at = c["nc"], c["sem"], c["at"]
    u, uf, xa, clo, cf, cl = (h[n] for n in ("u", "uf", "xa", "clo", "cf", "cl"))
    n_hop = 2 if two else 1
    step = n_hop * T
    with ExitStack() as st:
        ps = st.enter_context(nc.psum_tensor(f"{tag}_ps", [128, HB, BANK], F32))
        s_pe, s_clo, s_w, s_uf, s_hi, s_u = (sem(f"{tag}_{n}") for n in ("pe", "clo", "w", "uf", "hi", "u"))

        def loop(eng, one):
            if pairs == 1:
                for hop in range(n_hop):
                    for t in range(T):
                        one(hop, t, hop * T + t + 1)
            else:
                with eng.Fori(0, pairs) as i:
                    for hop in range(n_hop):
                        for t in range(T):
                            one(hop, t, i * step + (hop * T + t + 1))

        with nc.Block() as block:
            @block.gpsimd
            def _(pool):
                pool.sem_inc(s_u, T)
                pool.sem_inc(s_w, HB)

            @block.tensor
            def _(pe):
                def one(hop, t, n):
                    pe.wait_ge(s_w, n)
                    for k in range(T):
                        if t == 0:
                            pe.wait_ge(s_u, n + k)
                        last = pe.matmul(ps[:, t % HB, 0:2 * F], at[:, k, t * P:t * P + 128], u[hop][:, k, :],
                                         start=(k == 0), stop=(k == T - 1))
                    last.then_inc(s_pe, 1)
                loop(pe, one)

            @block.scalar
            def _(act):
                def one(hop, t, n):
                    b = t % HB
                    act.wait_ge(s_pe, n)
                    act.wait_ge(s_w, n)
                    act.activation(clo[:, b, :], ps[0:P, b, F:2 * F], ACT.Copy, scale=cl[:, t:t + 1]).then_inc(s_clo, 1)
                    act.wait_ge(s_uf, n)
                    act.activation(u[(hop + 1) % 2][:, t, 0:F], uf[:, t, :], ACT.Copy, scale=1.0 / LO).then_inc(s_hi, 1)
                loop(act, one)

            @block.vector
            def _(v):
                def one(hop, t, n):
                    b = t % HB
                    v.wait_ge(s_clo, n)
                    high = v.scalar_tensor_tensor(uf[:, t, :], ps[0:P, b, 0:F], cf[:, t:t + 1], clo[:, b, :],
                                                  ALU.mult, ALU.add)
                    high.then_inc(s_w, 1)
                    v.wait_ge(s_w, n + HB)
                    v.tensor_tensor(uf[:, t, :], uf[:, t, :], xa[:, t, :], ALU.add).then_inc(s_uf, 1)
                    v.wait_ge(s_hi, n)
                    v.scalar_tensor_tensor(u[(hop + 1) % 2][:, t, F:2 * F], u[(hop + 1) % 2][:, t, 0:F], -LO,
                                           uf[:, t, :], ALU.mult, ALU.add).then_inc(s_u, 1)
                loop(v, one)


def hop_result(c, tag, h, res, bias):
    nc, sem = c["nc"], c["sem"]
    with ExitStack() as st:
        s_ch, s_b = sem(f"{tag}_ch"), sem(f"{tag}_b")
        b = st.enter_context(nc.sbuf_tensor(f"{tag}_bias", [P, F], F32)) if bias else None
        with nc.Block() as block:
            if bias:
                @block.sync
                def _(sp):
                    sp.dma_start(b[:, :], c["w"][bias].rearrange("(o f) -> o f", o=1).to_broadcast([P, F])).then_inc(s_b, 16)

            @block.vector
            def _(v):
                ch = Chain(v, s_ch)
                ch(v.tensor_tensor(res[:, :, :], h["uf"][:, :, :], bc(c["dsqrt"][:, :], F), ALU.mult))
                if bias:
                    v.wait_ge(s_b, 16)
                    v.tensor_tensor(res[:, :, :], res[:, :, :], b[:, :].unsqueeze(1).to_broadcast([P, T, F]), ALU.add)


def rsqrt_steps(c, v, ch, act_sem, root_sem, var, y, e):
    v.sem_inc(act_sem, 1)
    v.wait_ge(root_sem, 1)
    ch(v.reciprocal(y, y))
    ch(v.tensor_tensor(e, y, y, ALU.mult))
    ch(v.tensor_tensor(e, e, var, ALU.mult))
    ch(v.tensor_scalar(e, e, -0.5, 1.5, ALU.mult, ALU.add))
    ch(v.tensor_tensor(y, y, e, ALU.mult))


def layer_norm(c, tag, xs, h, scr):
    nc, sem = c["nc"], c["sem"]
    with ExitStack() as st:
        mean, var, y, e = (st.enter_context(nc.sbuf_tensor(f"{tag}_{n}", [P, T], F32)) for n in ("mean", "var", "y", "e"))
        s_ch, s_var, s_root = sem(f"{tag}_ch"), sem(f"{tag}_var"), sem(f"{tag}_root")
        with nc.Block() as block:
            @block.scalar
            def _(act):
                act.wait_ge(s_var, 1)
                act.activation(y[:, :], var[:, :], ACT.Sqrt).then_inc(s_root, 1)

            @block.vector
            def _(v):
                ch = Chain(v, s_ch)
                ch(v.tensor_tensor(xs[:, :, :], xs[:, :, :], h[:, :, :], ALU.add))
                ch(v.reduce_sum(mean[:, :], xs[:, :, :], X_AXIS))
                ch(v.tensor_scalar(mean[:, :], mean[:, :], 1.0 / F, None, ALU.mult))
                ch(v.tensor_tensor(xs[:, :, :], xs[:, :, :], bc(mean[:, :], F), ALU.subtract))
                ch(v.tensor_tensor(scr[:, :, :], xs[:, :, :], xs[:, :, :], ALU.mult))
                ch(v.reduce_sum(var[:, :], scr[:, :, :], X_AXIS))
                ch(v.tensor_scalar(var[:, :], var[:, :], 1.0 / F, EPS, ALU.mult, ALU.add))
                rsqrt_steps(c, v, ch, s_var, s_root, var[:, :], y[:, :], e[:, :])
                v.tensor_tensor(xs[:, :, :], xs[:, :, :], bc(y[:, :], F), ALU.mult)


def graph_norm(c, tag, h, scr):
    nc, sem = c["nc"], c["sem"]
    with ExitStack() as st:
        def sb(name, shape):
            return st.enter_context(nc.sbuf_tensor(f"{tag}_{name}", shape, F32))
        wt, bi, ms = sb("wt", [P, F]), sb("bi", [P, F]), sb("ms", [P, F])
        s1, var, y, e, ones = sb("s1", [P, F]), sb("var", [P, F]), sb("y", [P, F]), sb("e", [P, F]), sb("ones", [P, P])
        ps = st.enter_context(nc.psum_tensor(f"{tag}_ps", [128, 2, BANK], F32))
        s_w, s_ch, s_part, s_sum, s_var, s_root = (sem(f"{tag}_{n}") for n in ("w", "ch", "part", "sum", "var", "root"))

        def rows(ap):
            return ap.unsqueeze(1).to_broadcast([P, T, F])
        with nc.Block() as block:
            @block.sync
            def _(sp):
                for sbuf, name in ((wt, "gn_weight"), (bi, "gn_bias"), (ms, "gn_scale")):
                    sp.dma_start(sbuf[:, :], c["w"][name].rearrange("(o f) -> o f", o=1).to_broadcast([P, F])).then_inc(s_w, 16)

            @block.tensor
            def _(pe):
                for i in range(2):
                    pe.wait_ge(s_part, i + 1)
                    pe.matmul(ps[0:P, i, 0:F], ones[:, :], s1[:, :], start=True, stop=True).then_inc(s_sum, 1)

            @block.scalar
            def _(act):
                act.wait_ge(s_var, 1)
                act.activation(y[:, :], var[:, :], ACT.Sqrt).then_inc(s_root, 1)

            @block.vector
            def _(v):
                ch = Chain(v, s_ch)
                v.memset(ones[:, :], 1.0)
                ch(v.reduce_sum(s1[:, :], h[:, :, :].rearrange("p t f -> p f t"), X_AXIS))
                v.sem_inc(s_part, 1)
                v.wait_ge(s_sum, 1)
                v.wait_ge(s_w, 48)
                ch(v.scalar_tensor_tensor(e[:, :], ps[0:P, 0, 0:F], 1.0 / N, ms[:, :], ALU.mult, ALU.mult))
                ch(v.tensor_tensor(h[:, :, :], h[:, :, :], rows(e[:, :]), ALU.subtract))
                ch(v.tensor_tensor(scr[:, :, :], h[:, :, :], h[:, :, :], ALU.mult))
                ch(v.reduce_sum(s1[:, :], scr[:, :, :].rearrange("p t f -> p f t"), X_AXIS))
                v.sem_inc(s_part, 1)
                v.wait_ge(s_sum, 2)
                ch(v.tensor_scalar(var[:, :], ps[0:P, 1, 0:F], 1.0 / N, EPS, ALU.mult, ALU.add))
                rsqrt_steps(c, v, ch, s_var, s_root, var[:, :], y[:, :], e[:, :])
                ch(v.tensor_tensor(y[:, :], y[:, :], wt[:, :], ALU.mult))
                ch(v.tensor_tensor(h[:, :, :], h[:, :, :], rows(y[:, :]), ALU.mult))
                ch(v.tensor_tensor(h[:, :, :], h[:, :, :], rows(bi[:, :]), ALU.add))
                v.tensor_scalar(h[:, :, :], h[:, :, :], 0.0, None, ALU.max)


def node_product(c, tag, xs, y, w1, w2, bias):
    nc, sem, ident = c["nc"], c["sem"], c["ident"]
    m = 2 * F if w2 else F
    with ExitStack() as st:
        def sb(name, shape):
            return st.enter_context(nc.sbuf_tensor(f"{tag}_{name}", shape, F32))
        wc = sb("w", [F, m])
        xt = sb("xt", [F, 2, 128])
        bi = sb("bi", [P, F]) if w2 else None
        root = sb("root", [P, T, F]) if w2 else None
        pt = st.enter_context(nc.psum_tensor(f"{tag}_pt", [128, 2, BANK], F32))
        py = st.enter_context(nc.psum_tensor(f"{tag}_py", [128, 2, BANK], F32))
        s_w, s_t, s_c, s_y, s_o, s_st = (sem(f"{tag}_{n}") for n in ("w", "t", "c", "y", "o", "st"))
        with nc.Block() as block:
            @block.sync
            def _(sp):
                sp.dma_start(wc[:, 0:F], c["w"][w1]).then_inc(s_w, 16)
                if w2:
                    sp.dma_start(wc[:, F:m], c["w"][w2]).then_inc(s_w, 16)
                    sp.dma_start(bi[:, :], c["w"][bias].rearrange("(o f) -> o f", o=1).to_broadcast([P, F])).then_inc(s_w, 16)
                    sp.wait_ge(s_o, T)
                    sp.dma_start(node_view(c["y_d"]), y[:, :, :]).then_inc(s_st, 16)
                    sp.dma_start(node_view(c["root_d"]), root[:, :, :]).then_inc(s_st, 16)
                    sp.wait_ge(s_st, 32)

            @block.tensor
            def _(pe):
                def turn(t):
                    if t >= 2:
                        pe.wait_ge(s_c, t - 1)
                    pe.transpose(pt[0:F, t % 2, 0:P], xs[:, t, :], ident[0:P, 0:P]).then_inc(s_t, 1)

                turn(0)
                pe.wait_ge(s_w, 48 if w2 else 16)
                for t in range(T):
                    if t + 1 < T:
                        turn(t + 1)
                    pe.wait_ge(s_c, t + 1)
                    if t >= 2:
                        pe.wait_ge(s_o, t - 1)
                    pe.matmul(py[0:P, t % 2, 0:m], xt[:, t % 2, 0:P], wc[:, :], start=True, stop=True).then_inc(s_y, 1)

            @block.scalar
            def _(act):
                for t in range(T):
                    act.wait_ge(s_t, t + 1)
                    if t >= 2:
                        act.wait_ge(s_y, t - 1)
                    act.copy(xt[:, t % 2, 0:P], pt[0:F, t % 2, 0:P]).then_inc(s_c, 1)

            @block.vector
            def _(v):
                for t in range(T):
                    v.wait_ge(s_y, t + 1)
                    if w2:
                        if t == 0:
                            v.wait_ge(s_w, 48)
                        v.tensor_tensor(root[:, t, :], py[0:P, t % 2, F:m], bi[:, :], ALU.add)
                    v.tensor_copy(y[:, t, :], py[0:P, t % 2, 0:F]).then_inc(s_o, 1)


def edge_conv(c, tag, src_cols, ea_t, w_edge):
    nc, ident = c["nc"], c["ident"]
    sems = []

    def sem(name):
        sems.append(nc.alloc_semaphore(name=name))
        return sems[-1]

    n_it = C // (G * G)
    slot = [q % 2 for q in range(G)]
    ago = [1, 3] + [2] * (G - 2)
    with ExitStack() as st:
        def sb(name, shape, dt):
            return st.enter_context(nc.sbuf_tensor(f"{tag}_{name}", shape, dt))
        gat = sb("gathered", [P, G, G, F], F32)
        idx_all = sb("idx_all", [P, C + G * G], I32)
        idx = sb("idx", [P, G, G], I32)
        comb = sb("scan_and_attr", [128, G, GE], F32)
        mk = sb("mask", [F, G, GE], BF16)
        back = sb("back", [P, G, G * F], F32)
        we = sb("we", [128, F], F32)
        msg = st.enter_context(nc.psum_tensor(f"{tag}_msg", [128, 2, 2, BANK], F32))
        tr = st.enter_context(nc.psum_tensor(f"{tag}_tr", [128, 2, BANK], F32))
        s_w, s_init, s_idx, s_msg, s_scan, s_half, s_tr, s_back, s_gate = (
            sem(f"{tag}_{n}") for n in ("w", "init", "idx", "msg", "scan", "half", "tr", "back", "gate"))
        s_gat, s_ea, s_mk, s_st = ([sem(f"{tag}_{n}{q}") for q in range(G)] for n in ("gat", "ea", "mk", "st"))
        scan_v = c["scan_d"].rearrange("(g j p) f -> g p j f", j=G, p=P)

        with nc.Block() as block:
            @block.sync
            def _(sp):
                sp.dma_start(idx_all[:, 0:C], src_cols).then_inc(s_w, 16)
                sp.dma_start(we[F:128, :], c["w"][w_edge]).then_inc(s_w, 16)
                with sp.Fori(0, n_it) as i:
                    for q in range(G):
                        n = i * G + q
                        sp.wait_ge(s_msg, n + 1)
                        sp.sem_inc(s_gate, 1)
                        sp.dma_start(comb[F:128, q, :], ea_t[:, bass.ds(n * GE, GE)]).then_inc(s_ea[q], 16)
                        sp.wait_ge(s_scan, n + 1)
                        sp.sem_inc(s_gate, 1)
                        sp.dma_start(mk[:, q, :], c["mask_d"][:, bass.ds(n * GE, GE)].to_broadcast([F, GE])).then_inc(s_mk[q], 16)

            @block.gpsimd
            def _(pool):
                for s in (s_msg, s_scan, s_tr, s_back):
                    pool.sem_inc(s, G)
                for s in s_st:
                    pool.sem_inc(s, 16)
                with pool.Fori(0, n_it) as i:
                    for q in range(G):
                        n = i * G + q
                        pool.wait_ge(s_msg, n + 1)
                        pool.wait_ge(s_idx, n + 1)
                        pool.sem_inc(s_gate, 1)
                        for j in range(G):
                            pool.indirect_dma_start(
                                out=gat[:, q, j, :], out_offset=None, in_=c["y_d"],
                                in_offset=bass.IndirectOffsetOnAxis(ap=idx[:, q, j:j + 1], axis=0),
                            ).then_inc(s_gat[q], 16)

            @block.tensor
            def _(pe):
                def messages(i, q):
                    n = i * G + q
                    pe.wait_ge(s_scan, n + (G + 1 - ago[q]))
                    pe.wait_ge(s_ea[q], 16 * i + 16)
                    pe.wait_ge(s_gat[q], 16 * G * i + 16 * G)
                    for j in range(G):
                        b, o = divmod(j, BLK)
                        at = msg[0:F, slot[q], b, o * P:(o + 1) * P]
                        pe.matmul(at, gat[:, q, j, :], ident[0:P, 0:P], start=True, stop=False)
                        last = pe.matmul(at, we[F:128, :], comb[F:128, q, j * P:(j + 1) * P], start=False, stop=True)
                    last.then_inc(s_msg, 1)

                def turn_back(i, q):
                    n = i * G + q
                    pe.wait_ge(s_back, n + (G + 1 - ago[q]))
                    pe.wait_ge(s_scan, n + (G + 1))
                    for j in range(G):
                        last = pe.transpose(tr[0:P, slot[q], j * F:(j + 1) * F], comb[0:F, q, j * P:(j + 1) * P],
                                            ident[0:F, 0:F])
                    last.then_inc(s_tr, 1)

                pe.wait_ge(s_w, 32)
                with pe.Fori(0, n_it) as i:
                    messages(i, 0)
                    for q in range(1, G):
                        messages(i, q)
                        turn_back(i, q - 1)
                    turn_back(i, G - 1)

            @block.vector
            def _(v):
                v.memset(idx_all[:, C:C + G * G], 0)
                v.memset(comb[0:F, G - 1, GE - 1:GE], 0.0).then_inc(s_init, 1)
                v.wait_ge(s_init, 1)
                v.wait_ge(s_w, 32)
                for q in range(G):
                    v.tensor_copy(idx[:, q, :], idx_all[:, q * G:(q + 1) * G]).then_inc(s_idx, 1)
                with v.Fori(0, n_it) as i:
                    for q in range(G):
                        n = i * G + q
                        v.wait_ge(s_mk[q], 16 * i + 16)
                        v.wait_ge(s_tr, n + 1)
                        v.wait_ge(s_scan, n + G)
                        v.wait_ge(s_msg, n + (G + 1))
                        v.tensor_tensor_scan(comb[0:F, q, 0:GE - P], mk[:, q, 0:GE - P], msg[0:F, slot[q], 0, 0:GE - P],
                                             comb[0:F, (q - 1) % G, GE - 1:GE], ALU.add, ALU.max).then_inc(s_half, 1)
                        v.wait_ge(s_half, n + 1)
                        v.tensor_tensor_scan(comb[0:F, q, GE - P:GE], mk[:, q, GE - P:GE], msg[0:F, slot[q], 1, 0:P],
                                             comb[0:F, q, GE - P - 1:GE - P], ALU.add, ALU.max).then_inc(s_scan, 1)
                        v.tensor_copy(idx[:, q, :], idx_all[:, bass.ds((n + G) * G, G)]).then_inc(s_idx, 1)

            @block.scalar
            def _(act):
                with act.Fori(0, n_it) as i:
                    for q in range(G):
                        n = i * G + q
                        act.wait_ge(s_st[q], 16 * i + 16)
                        act.wait_ge(s_tr, n + (G + 1))
                        act.copy(back[:, q, :], tr[0:P, slot[q], 0:G * F]).then_inc(s_back, 1)
                        act.wait_ge(s_back, n + (G + 1))
                        act.dma_start(scan_v[bass.ds(n, 1), :, :, :].rearrange("o p j f -> (o p) j f"),
                                      back[:, q, :].rearrange("p (j f) -> p j f", f=F)).then_inc(s_st[q], 16)
                for q in range(G):
                    act.wait_ge(s_st[q], 16 * n_it + 16)
    nc.clear_and_free_semaphores(sems)
    nc.all_engine_barrier()


def conv_result(c, tag, res):
    nc, sem = c["nc"], c["sem"]
    with ExitStack() as st:
        root = st.enter_context(nc.sbuf_tensor(f"{tag}_root", [P, T, F], F32))
        s_g, s_r, s_ch = sem(f"{tag}_g"), sem(f"{tag}_r"), sem(f"{tag}_ch")
        with nc.Block() as block:
            @block.gpsimd
            def _(pool):
                for t in range(T):
                    pool.indirect_dma_start(out=res[:, t, :], out_offset=None, in_=c["scan_d"],
                                            in_offset=bass.IndirectOffsetOnAxis(ap=c["end_idx"][:, t:t + 1], axis=0),
                                            ).then_inc(s_g, 16)

            @block.sync
            def _(sp):
                sp.dma_start(root[:, :, :], node_view(c["root_d"])).then_inc(s_r, 16)

            @block.vector
            def _(v):
                ch = Chain(v, s_ch)
                v.wait_ge(s_r, 16)
                v.wait_ge(s_g, 16 * T)
                ch(v.tensor_tensor(res[:, :, :], res[:, :, :], bc(c["has_in"][:, :], F), ALU.mult))
                ch(v.tensor_tensor(root[:, :, :], root[:, :, :], res[:, :, :], ALU.add))
                v.scalar_tensor_tensor(res[:, :, :], root[:, :, :], 0.01, root[:, :, :], ALU.mult, ALU.max)


_WEIGHTS = {"W1_msg": "L1_gnn_W1_msg", "W1_edge": "L1_gnn_W1_edge", "W1_root": "L1_gnn_W1_root", "b1": "L1_gnn_b1",
            "W2_msg": "L1_gnn_W2_msg", "W2_edge": "L1_gnn_W2_edge", "W2_root": "L1_gnn_W2_root", "b2": "L1_gnn_b2",
            "g_W1": "L3_gnn_W1", "g_b1": "L3_gnn_b1", "gn_weight": "L3_gnn_gn_weight", "gn_bias": "L3_gnn_gn_bias",
            "gn_scale": "L3_gnn_gn_mean_scale", "g_W2": "L3_gnn_W2", "g_b2": "L3_gnn_b2"}


def kernel(**inputs):
    import numpy as np
    import concourse.bacc as bacc
    from concourse.bass_utils import run_bass_kernel_spmd

    nc = bacc.Bacc("TRN2", target_bir_lowering=False, num_devices=1)
    src = np.asarray(inputs["src"])
    arrays = {
        "x": np.ascontiguousarray(inputs["x"]),
        "src": np.ascontiguousarray(src),
        "dst": np.ascontiguousarray(inputs["dst"]),
        "src_cols": np.ascontiguousarray(src.reshape(C, P).T),
        "ea_t": np.ascontiguousarray(np.asarray(inputs["edge_attr_32"]).T),
    }
    for short, name in _WEIGHTS.items():
        arrays["w_" + short] = np.ascontiguousarray(inputs[name])
    aps = {n: nc.dram_tensor("in_" + n, a.shape, mybir.dt.from_np(a.dtype), kind="ExternalInput").ap()
           for n, a in arrays.items()}
    out = nc.dram_tensor("out_x", (N, F), F32, kind="ExternalOutput").ap()
    build(nc, aps["x"], aps["src"], aps["dst"], aps["src_cols"], aps["ea_t"], {n: aps["w_" + n] for n in _WEIGHTS}, out)
    r = run_bass_kernel_spmd(nc, [{"in_" + n: a for n, a in arrays.items()}], core_ids=[0])
    return r.results[0]["out_x"]
```

```python
import concourse.bass as bass
from concourse import mybir
from contextlib import ExitStack

F32 = mybir.dt.float32
F16 = mybir.dt.float16
BF16 = mybir.dt.bfloat16
I32 = mybir.dt.int32
ALU = mybir.AluOpType
ACT = mybir.ActivationFunctionType
X_AXIS = mybir.AxisListType.X

N, F, DE, E = 3125, 96, 32, 53125
P = 125
T = N // P
C = E // P
LO = 2048.0
NEG = -3.0e38
MAGIC = 1.5 * 2.0 ** 23
K = 128
W = 25
S = P // W
NW = N // W
WK = -(-E // (NW * K))
WIN = WK * K
HOTW = T * W + 1
ATW = N + 3
BLK = 4
BANK = 512
G = 5
GE = G * P
HB = 5
EPS = 1e-5


class Chain:

    def __init__(self, eng, sem):
        self.eng, self.sem, self.n = eng, sem, 0

    def __call__(self, ins):
        self.n += 1
        ins.then_inc(self.sem, 1)
        self.eng.wait_ge(self.sem, self.n)


def build(nc, x, src, dst, src_cols, ea_t, w, out):
    top = ExitStack()
    with top:
        def keep(name, shape, dt):
            return top.enter_context(nc.sbuf_tensor(name, shape, dt))

        def sem(name):
            return top.enter_context(nc.semaphore(name))

        at = keep("counts", [P, T, ATW], F16)
        ident = keep("ident", [128, 128], F32)
        ident16 = keep("ident16", [P, 2, P], F16)
        dinv = keep("dinv", [P, T], F32)
        dinv_lo = keep("dinv_lo", [P, T], F32)
        dsqrt = keep("dsqrt", [P, T], F32)
        has_in = keep("has_in", [P, T], F32)
        end_idx = keep("end_idx", [P, T], I32)
        start_f = keep("start_f", [1, T], F32)

        ev_d = nc.dram_tensor("edge_values", (E + WIN, 3), F32).ap()
        mask_d = nc.dram_tensor("segment_mask", (1, E), BF16).ap()
        y_d = nc.dram_tensor("messages", (N, 2 * F), F16).ap()
        root_d = nc.dram_tensor("root_parked", (N, F), F32).ap()
        scan_d = nc.dram_tensor("running_max", (E, F), F32).ap()
        ctx = dict(nc=nc, sem=sem, at=at, ident=ident, ident16=ident16, dinv=dinv, dinv_lo=dinv_lo, dsqrt=dsqrt, has_in=has_in,
                   end_idx=end_idx, start_f=start_f, ev_d=ev_d, mask_d=mask_d, y_d=y_d,
                   root_d=root_d, scan_d=scan_d, w=w)
        xs = keep("x_state", [P, T, F], F32)
        ctx["x_loaded"] = x_loaded = sem("x_loaded")
        build_counts(ctx, src, dst, xs, x)
        degrees(ctx)
        with ExitStack() as st:
            hs = hop_state(ctx, st, "l0")
            hops(ctx, "l0", hs, xs, 1.0, 0.0, 0, 2, norm=xs)
        node_product(ctx, "c1w", xs, "W1_msg", "W1_root", "b1")
        edge_conv(ctx, "c1", src_cols, ea_t, "W1_edge")
        with ExitStack() as st:
            c1 = st.enter_context(nc.sbuf_tensor("c1", [P, T, F], F32))
            conv_result(ctx, "c1r", c1, None)
            node_product(ctx, "c2w", c1, "W2_msg", "W2_root", "b2")
        edge_conv(ctx, "c2", src_cols, ea_t, "W2_edge")
        with ExitStack() as st:
            c2 = st.enter_context(nc.sbuf_tensor("c2", [P, T, F], F32))
            conv_result(ctx, "c2r", c2, xs)
        with ExitStack() as st:
            hs = hop_state(ctx, st, "l2")
            h = hs["uf"]
            hops(ctx, "l2", hs, xs, 0.9, 0.1, 7, 2, norm=xs)
            node_product(ctx, "g1w", xs, "g_W1", hs=hs)
            hops(ctx, "g1", hs, h, 1.0, 0.0, 0, 1, bias="g_b1")
            node_product(ctx, "g2w", h, "g_W2", hs=hs, graph_norm=True)
            hops(ctx, "g2", hs, h, 1.0, 0.0, 0, 1, bias="g_b2", norm=xs, out=out)


def bc(ap, n):
    return ap.unsqueeze(2).to_broadcast([ap.shape[0], ap.shape[1], n])


def node_view(dram):
    return dram.rearrange("(t p) f -> p t f", p=P)


def build_counts(c, src, dst, xs, x):
    nc = c["nc"]
    with ExitStack() as st:
        def sb(name, shape, dt):
            return st.enter_context(nc.sbuf_tensor(name, shape, dt))
        tab = dict(iota=sb("iota", [K, HOTW], F16), wbase=sb("wbase", [K, NW], F32), start_i=sb("start_i", [1, NW], I32))
        with ExitStack() as s1:
            edge_values(c, s1, src, dst, tab, xs, x)
        with ExitStack() as s1:
            table_rounds(c, s1, tab)


def edge_values(c, st, src, dst, tab, xs, x):
    nc, sem, ident = c["nc"], c["sem"], c["ident"]

    def sb(name, shape, dt):
        return st.enter_context(nc.sbuf_tensor(name, shape, dt))

    di, si, pv = sb("di", [P, C], I32), sb("si", [P, C], I32), sb("pv", [P, 1], I32)
    ev = sb("ev", [P, C, 3], F32)
    dstf, srcf, pvf = sb("dstf", [P, C], F32), sb("srcf", [P, C], F32), sb("pvf", [P, 1], F32)
    tile16, sub16 = sb("tile16", [P, C], F16), sb("sub16", [P, C], F16)
    tmp, neq = sb("tmp", [P, C], F32), sb("neq", [P, C], F32)
    mask = sb("mask", [P, C], BF16)
    pidx, fidx = sb("pidx", [K, 1], F32), sb("fidx", [K, K], F32)
    i25 = sb("i25", [P, T], F16)
    flat = c["at"][:, :, :].rearrange("p t d -> p (t d)")
    hot_t = flat[:, 0:C * T].rearrange("p (c t) -> p c t", t=T)
    hot_s = flat[:, C * T + 1:C * (T + S) + 1].rearrange("p (c s) -> p c s", s=S)
    same = sb("same", [P, G, S], F32)
    part, pair = sb("part", [P, G], F32), sb("pair", [P, G, S], F32)
    blk, tl, bin_no = sb("blk", [P, 1], F32), sb("tl", [P, 1], F32), sb("bin_no", [P, S], F32)
    before = sb("before", [P, S, NW], F32)
    hist = sb("hist", [P, S], F32)
    pad = sb("pad", [K, 3 * WK], F32)
    ps = st.enter_context(nc.psum_tensor("hist_ps", [128, BANK], F32))
    ps2 = st.enter_context(nc.psum_tensor("start_ps", [128, BANK], F32))
    s_dst, s_src, s_prev, s_iota, s_ch = (sem(f"k_{n}") for n in ("dst", "src", "prev", "iota", "chain"))
    s_ev, s_mask, s_hot, s_hist, s_part, s_start, s_store = (
        sem(f"k_{n}") for n in ("ev", "mask", "hot", "hist", "part", "start", "store"))
    dst_v, src_v = (a.rearrange("(p c) -> p c", p=P) for a in (dst, src))
    ev_flat = c["ev_d"].rearrange("e a -> (e a)")

    with nc.Block() as block:
        @block.sync
        def _(sp):
            sp.dma_start(di[:, :], dst_v).then_inc(s_dst, 16)
            sp.dma_start(si[:, :], src_v).then_inc(s_src, 16)
            sp.dma_start(xs[:, :, :], node_view(x)).then_inc(c["x_loaded"], 16)
            sp.wait_ge(s_ev, 1)
            sp.dma_start(ev_flat[0:3 * E].rearrange("(p c) -> p c", p=P), ev[:, :, :].rearrange("p c a -> p (c a)")).then_inc(s_store, 16)
            sp.dma_start(ev_flat[3 * E:3 * (E + WIN)].rearrange("(p c) -> p c", p=K), pad[:, :]).then_inc(s_store, 16)
            sp.wait_ge(s_mask, 1)
            sp.dma_start(c["mask_d"].rearrange("o (p c) -> (o p) c", p=P), mask[:, :]).then_inc(s_store, 16)
            sp.wait_ge(s_store, 48)
            sp.wait_ge(c["x_loaded"], 16)

        @block.scalar
        def _(act):
            act.wait_ge(s_iota, 1)
            with nc.allow_non_contiguous_dma(reason="the last dst of each partition, single values"):
                act.dma_start(pv[1:P, 0:1], dst_v[0:P - 1, C - 1:C]).then_inc(s_prev, 16)
            act.wait_ge(s_prev, 16)

        @block.gpsimd
        def _(pool):
            pool.memset(pv[:, :], -1).then_inc(s_iota, 1)
            pool.iota(i25[:, :], pattern=[[1, T]], base=0, channel_multiplier=0,
                      allow_small_or_imprecise_dtypes=True).then_inc(s_iota, 1)
            pool.iota(pidx[:, :], pattern=[[0, 1]], base=0, channel_multiplier=1,
                      allow_small_or_imprecise_dtypes=True).then_inc(s_iota, 1)
            pool.iota(fidx[:, :], pattern=[[1, K]], base=0, channel_multiplier=0,
                      allow_small_or_imprecise_dtypes=True).then_inc(s_iota, 1)
            pool.iota(tab["iota"][:, :], pattern=[[1, HOTW]], base=0, channel_multiplier=0,
                      allow_small_or_imprecise_dtypes=True).then_inc(s_iota, 1)
            pool.iota(tab["wbase"][:, :], pattern=[[W, NW]], base=0, channel_multiplier=0,
                      allow_small_or_imprecise_dtypes=True).then_inc(s_iota, 1)

        @block.vector
        def _(v):
            ch = Chain(v, s_ch)

            def tile_of(out, a, size):
                ch(v.tensor_scalar(out, a, float(size // 2), 1.0 / size, ALU.subtract, ALU.mult))
                ch(v.tensor_scalar(out, out, MAGIC, MAGIC, ALU.add, ALU.subtract))

            v.memset(pad[:, :], -1.0)
            v.wait_ge(s_iota, 4)
            v.tensor_scalar(ident[:, :], fidx[:, :], pidx[:, :], None, ALU.is_equal)
            tile_of(blk[:, :], pidx[0:P, :], T)
            ch(v.scalar_tensor_tensor(tl[:, :], blk[:, :], -float(T), pidx[0:P, :], ALU.mult, ALU.add))
            for b in range(G):
                v.tensor_scalar(same[:, b, :], blk[:, :].to_broadcast([P, S]), float(b), None, ALU.is_equal)
                v.tensor_scalar(bin_no[:, b:b + 1], tl[:, :], float(S), float(b), ALU.mult, ALU.add)
            ch(v.memset(part[:, :], 0.0))
            for b in range(S):
                v.tensor_scalar(before[:, b, :], fidx[0:P, 0:NW], bin_no[:, b:b + 1], None, ALU.is_gt)
            v.wait_ge(s_dst, 16)
            ch(v.tensor_copy(dstf[:, :], di[:, :]))
            tile_of(tmp[:, :], dstf[:, :], P)
            ch(v.tensor_copy(tile16[:, :], tmp[:, :]))
            v.tensor_tensor(hot_t[:, :, :], bc(tile16[:, :], T), i25[:, :].unsqueeze(1).to_broadcast([P, C, T]), ALU.is_equal)
            ch(v.scalar_tensor_tensor(tmp[:, :], tmp[:, :], -float(P), dstf[:, :], ALU.mult, ALU.add))
            tile_of(tmp[:, :], tmp[:, :], W)
            ch(v.tensor_copy(sub16[:, :], tmp[:, :]))
            v.tensor_tensor(hot_s[:, :, :], bc(sub16[:, :], S), i25[:, 0:S].unsqueeze(1).to_broadcast([P, C, S]),
                            ALU.is_equal).then_inc(s_hot, 1)
            v.wait_ge(s_src, 16)
            v.tensor_copy(ev[:, :, 2], dstf[:, :])
            ch(v.tensor_copy(srcf[:, :], si[:, :]))
            tile_of(tmp[:, :], srcf[:, :], P)
            v.scalar_tensor_tensor(ev[:, :, 1], tmp[:, :], -float(P), srcf[:, :], ALU.mult, ALU.add)
            v.scalar_tensor_tensor(ev[:, :, 0], tmp[:, :], float(W), dstf[:, :], ALU.mult, ALU.add).then_inc(s_ev, 1)
            v.wait_ge(s_hist, 1)
            ch(v.tensor_tensor(pair[:, :, :], ps[0:P, 0:G * S].rearrange("p (b s) -> p b s", s=S), same[:, :, :], ALU.mult))
            v.reduce_sum(hist[:, :], pair[:, :, :].rearrange("p b s -> p s b"), X_AXIS).then_inc(s_part, 1)
            v.wait_ge(s_start, 1)
            v.tensor_copy(tab["start_i"][:, :], ps2[0:1, 0:NW])
            v.tensor_copy(c["start_f"][:, :], ps2[0:1, 0:NW].rearrange("o (t s) -> o t s", s=S)[:, :, 0])
            v.wait_ge(s_prev, 16)
            ch(v.tensor_copy(pvf[:, :], pv[:, :]))
            v.tensor_tensor(neq[:, 1:C], dstf[:, 1:C], dstf[:, 0:C - 1], ALU.not_equal)
            ch(v.tensor_tensor(neq[:, 0:1], dstf[:, 0:1], pvf[:, :], ALU.not_equal))
            v.tensor_scalar(mask[:, :], neq[:, :], NEG, None, ALU.mult).then_inc(s_mask, 1)

        @block.tensor
        def _(pe):
            pe.wait_ge(s_hot, 1)
            for g in range(C // G):
                last = pe.matmul(ps[0:P, 0:G * S], hot_t[:, g * G:(g + 1) * G, :].rearrange("p c t -> p (c t)"),
                                 hot_s[:, g * G:(g + 1) * G, :].rearrange("p c s -> p (c s)"),
                                 start=(g == 0), stop=(g == C // G - 1))
            last.then_inc(s_hist, 1)
            pe.wait_ge(s_part, 1)
            for b in range(S):
                last = pe.matmul(ps2[0:1, 0:NW], hist[:, b:b + 1], before[:, b, :], start=(b == 0), stop=(b == S - 1))
            last.then_inc(s_start, 1)


def table_rounds(c, st, tab):
    nc, sem, at, iota, wbase, start_i = c["nc"], c["sem"], c["at"], tab["iota"], tab["wbase"], tab["start_i"]

    def sb(name, shape, dt):
        return st.enter_context(nc.sbuf_tensor(name, shape, dt))
    hot = sb("hot", [K, S, WK, HOTW], F16)
    low = sb("low_hot", [K, S, WK, 128], F16)
    win = sb("win", [K, NW, WK, 3], F32)
    key, lkey, far = (sb(n, [K, S, WK], F32) for n in ("key", "low_key", "far"))
    ps = st.enter_context(nc.psum_tensor("count_ps", [128, 4, 2, BANK], F32))
    s_gate, s_key, s_hot, s_bank, s_flush = (sem(f"t_{n}") for n in ("gate", "key", "hot", "bank", "flush"))
    s_win = [sem(f"t_win{q}") for q in range(S)]
    slot = [q % 4 for q in range(S)]
    ago = [1] + [4] * (S - 1)
    FIRST = BLK * P

    with nc.Block() as block:
        def load_windows(eng, mine):
            def load(q, n):
                first = eng.value_load(start_i[0:1, bass.ds(n, 1)], min_val=0, max_val=E)
                eng.dma_start(win[:, bass.ds(n, 1), :, :].rearrange("p o k a -> p (o k a)"),
                              c["ev_d"][bass.ds(first, WIN), :].rearrange("(p k) a -> p (k a)", p=K)).then_inc(s_win[q], 16)
            for q in mine:
                load(q, q)
            with eng.Fori(1, T) as t:
                for q in mine:
                    eng.wait_ge(s_win[q], 16 * t)
                    eng.sem_inc(s_gate, 1)
                    load(q, t * S + q)

        @block.sync
        def _(sp):
            load_windows(sp, range(0, S, 2))

        @block.vector
        def _(v):
            v.memset(at[:, :, N:ATW], 0.0)
            with v.Fori(0, T) as t:
                for q in range(S):
                    v.wait_ge(s_win[q], 16 * t + 16)
                def mine(a):
                    return win[:, bass.ds(t * S, S), :, a]
                base = bc(wbase[:, bass.ds(t * S, S)], WK)
                v.wait_ge(s_hot, t * S + 1)
                v.tensor_tensor(key[:, :, :], mine(0), base, ALU.subtract)
                v.tensor_tensor(far[:, :, :], mine(2), base, ALU.subtract).then_inc(s_key, 1)
                v.wait_ge(s_key, 5 * t + 1)
                v.tensor_scalar(lkey[:, :, :], far[:, :, :], float(W - 1), None, ALU.subtract).then_inc(s_key, 1)
                v.wait_ge(s_key, 5 * t + 2)
                v.scalar_tensor_tensor(far[:, :, :], far[:, :, :], -1.0, lkey[:, :, :], ALU.mult, ALU.max).then_inc(s_key, 1)
                v.wait_ge(s_key, 5 * t + 3)
                v.tensor_scalar(far[:, :, :], far[:, :, :], 0.0, 128.0, ALU.max, ALU.mult).then_inc(s_key, 1)
                v.wait_ge(s_key, 5 * t + 4)
                v.tensor_tensor(lkey[:, :, :], far[:, :, :], mine(1), ALU.add).then_inc(s_key, 1)
                v.wait_ge(s_key, 5 * t + 5)
                for q in range(S):
                    v.wait_ge(s_bank, S * t + q + 1)
                    for k in range(WK):
                        v.tensor_scalar(low[:, q, k, :], iota[:, 0:128], lkey[:, q, k:k + 1], None, ALU.is_equal)
                        last = v.tensor_scalar(hot[:, q, k, :], iota[:, :], key[:, q, k:k + 1], None, ALU.is_equal)
                    last.then_inc(s_hot, 1)

        @block.tensor
        def _(pe):
            with pe.Fori(0, T) as t:
                for q in range(S):
                    n = t * S + q
                    pe.wait_ge(s_flush, n + (S + 1 - ago[q]))
                    pe.wait_ge(s_hot, n + 2)
                    for k in range(WK):
                        for b, (lo, hi) in enumerate(((0, FIRST), (FIRST, T * W))):
                            last = pe.matmul(ps[:, slot[q], b, 0:hi - lo], low[:, q, k, :], hot[:, q, k, lo:hi],
                                             start=(k == 0), stop=(k == WK - 1))
                    last.then_inc(s_bank, 1)

        @block.scalar
        def _(act):
            with act.Fori(0, T) as t:
                for q in range(S):
                    n = t * S + q
                    act.wait_ge(s_bank, n + (S + 1))
                    where = bass.ds(n * W, W)
                    act.copy(at[:, 0:FIRST // W, where],
                             ps[0:P, slot[q], 0, 0:FIRST].rearrange("p (h d) -> p h d", d=W))
                    act.copy(at[:, FIRST // W:T, where],
                             ps[0:P, slot[q], 1, 0:T * W - FIRST].rearrange("p (h d) -> p h d", d=W)).then_inc(s_flush, 1)

        @block.gpsimd
        def _(pool):
            pool.sem_inc(s_hot, 1)
            pool.sem_inc(s_bank, S)
            pool.sem_inc(s_flush, S)
            load_windows(pool, range(1, S, 2))


def degrees(c):
    nc, sem, at, ident = c["nc"], c["sem"], c["at"], c["ident"]
    with ExitStack() as st:
        def sb(name, shape, dt):
            return st.enter_context(nc.sbuf_tensor(name, shape, dt))
        ones = sb("deg_ones", [P, 2], F16)
        tri, pidx, fidx = sb("tri", [P, P], F32), sb("d_pidx", [P, 1], F32), sb("d_fidx", [P, P], F32)
        one_row = sb("one_row", [1, P], F32)
        deg, loops, y, e, root = (sb(f"d_{n}", [P, T], F32) for n in ("deg", "loops", "y", "e", "root"))
        ps = st.enter_context(nc.psum_tensor("deg_ps", [128, BANK], F32))
        ps2 = st.enter_context(nc.psum_tensor("end_ps", [128, BANK], F32))
        s_one, s_deg, s_ch, s_end, s_iota, s_root = (sem(f"d_{n}") for n in ("one", "deg", "chain", "end", "iota", "root"))
        s_degc, s_sq = sem("d_degc"), sem("d_sq")
        with nc.Block() as block:
            @block.gpsimd
            def _(pool):
                pool.iota(pidx[:, :], pattern=[[0, 1]], base=0, channel_multiplier=1,
                          allow_small_or_imprecise_dtypes=True).then_inc(s_iota, 1)
                pool.iota(fidx[:, :], pattern=[[1, P]], base=0, channel_multiplier=0,
                          allow_small_or_imprecise_dtypes=True).then_inc(s_iota, 1)

            @block.tensor
            def _(pe):
                pe.wait_ge(s_one, 1)
                for t in range(T):
                    for k in range(T):
                        last = pe.matmul(ps[:, t:t + 1], at[:, k, t * P:t * P + 128], ones[:, 0:1],
                                         start=(k == 0), stop=(k == T - 1))
                last.then_inc(s_deg, 1)
                pe.wait_ge(s_degc, 1)
                pe.matmul(ps2[0:P, 0:T], tri[:, :], deg[:, :], start=True, stop=False)
                pe.matmul(ps2[0:P, 0:T], one_row[:, :], c["start_f"][:, :], start=False, stop=True).then_inc(s_end, 1)

            @block.scalar
            def _(act):
                act.wait_ge(s_sq, 1)
                act.activation(root[:, :], loops[:, :], ACT.Sqrt).then_inc(s_root, 1)

            @block.vector
            def _(v):
                ch = Chain(v, s_ch)
                v.memset(ones[:, :], 1.0).then_inc(s_one, 1)
                v.memset(one_row[:, :], 1.0)
                v.wait_ge(s_iota, 2)
                v.tensor_scalar(tri[:, :], fidx[:, :], pidx[:, :], None, ALU.is_ge)
                v.wait_ge(s_deg, 1)
                ch(v.tensor_copy(deg[:, :], ps[0:P, 0:T]))
                v.sem_inc(s_degc, 1)
                v.tensor_scalar(c["has_in"][:, :], deg[:, :], 1.0, None, ALU.min)
                v.tensor_scalar(loops[:, :], deg[:, :], 1.0, None, ALU.add).then_inc(s_sq, 1)
                v.wait_ge(s_sq, 1)
                flat = at[:, :, :].rearrange("p t d -> p (t d)")
                for k in range(T):
                    a = flat[:, k * (ATW + P):k * (ATW + P) + P]
                    v.tensor_tensor(a, a, ident[0:P, 0:P], ALU.add)
                v.wait_ge(s_root, 1)
                ch(v.reciprocal(y[:, :], root[:, :]))
                ch(v.tensor_tensor(e[:, :], y[:, :], y[:, :], ALU.mult))
                ch(v.tensor_tensor(e[:, :], e[:, :], loops[:, :], ALU.mult))
                ch(v.tensor_scalar(e[:, :], e[:, :], -0.5, 1.5, ALU.mult, ALU.add))
                ch(v.tensor_tensor(c["dinv"][:, :], y[:, :], e[:, :], ALU.mult))
                v.tensor_scalar(c["dinv_lo"][:, :], c["dinv"][:, :], LO, None, ALU.mult)
                v.tensor_copy(c["ident16"][:, 0, :], ident[0:P, 0:P])
                v.tensor_scalar(c["ident16"][:, 1, :], ident[0:P, 0:P], 1.0 / LO, None, ALU.mult)
                v.scalar_tensor_tensor(c["dsqrt"][:, :], loops[:, :], 1.0 / LO, c["dinv"][:, :], ALU.mult, ALU.mult)
                v.wait_ge(s_end, 1)
                ch(v.tensor_scalar(e[:, :], ps2[0:P, 0:T], 1.0, 0.0, ALU.subtract, ALU.max))
                v.tensor_copy(c["end_idx"][:, :], e[:, :])


def row_vector(c, name, n):
    return c["w"][name].rearrange("(o f) -> o f", o=1).to_broadcast([n, F])


def hop_state(c, st, tag):
    nc = c["nc"]

    def sb(name, shape, dt):
        return st.enter_context(nc.sbuf_tensor(f"{tag}_{name}", shape, dt))

    wide = sb("wide", [P, N], F32)
    return dict(u=[sb("u0", [P, T, 2 * F], F16), sb("u1", [P, T, 2 * F], F16)], uf=sb("uf", [P, T, F], F32),
                wide=wide, xa=wide[:, 0:T * F].rearrange("p (t f) -> p t f", f=F), clo=sb("clo", [P, HB, F], F32),
                cf=sb("cf", [P, T], F32), cl=sb("cl", [P, T], F32))


class RowNorm:

    def __init__(self, c, st, tag, xs, sq, n=G):
        self.c, self.xs, self.n = c, xs, n
        nc = c["nc"]
        self.sq = sq
        self.mean, self.var, self.y, self.e = (
            st.enter_context(nc.sbuf_tensor(f"{tag}_{k}", [P, n], F32)) for k in ("mean", "var", "y", "e"))
        self.s_mid, self.s_sq, self.s_var, self.s_root = (c["sem"](f"{tag}_{k}") for k in ("mid", "sq", "var", "root"))
        self.groups = 0

    def vector(self, v, ch, g, h):
        x = self.xs[:, g * self.n:(g + 1) * self.n, :]
        sq = self.sq
        mean, var, y, e = (a[:, :] for a in (self.mean, self.var, self.y, self.e))
        ch(v.tensor_tensor(x, x, h, ALU.add))
        ch(v.reduce_sum(mean, x, X_AXIS))
        ch(v.tensor_scalar(mean, mean, 1.0 / F, None, ALU.mult))
        v.tensor_tensor(x, x, bc(mean, F), ALU.subtract).then_inc(self.s_mid, 1)
        v.wait_ge(self.s_sq, g + 1)
        ch(v.reduce_sum(var, sq, X_AXIS))
        v.tensor_scalar(var, var, 1.0 / F, EPS, ALU.mult, ALU.add).then_inc(self.s_var, 1)
        v.wait_ge(self.s_root, g + 1)
        ch(v.reciprocal(y, y))
        newton(v, ch, y, e, var)
        return v.tensor_tensor(x, x, bc(y, F), ALU.mult)

    def scalar(self, act, g):
        act.wait_ge(self.s_mid, g + 1)
        act.activation(self.sq, self.xs[:, g * self.n:(g + 1) * self.n, :], ACT.Square).then_inc(self.s_sq, 1)
        act.wait_ge(self.s_var, g + 1)
        act.activation(self.y[:, :], self.var[:, :], ACT.Sqrt).then_inc(self.s_root, 1)


def newton(v, ch, y, e, d):
    ch(v.tensor_tensor(e, y, y, ALU.mult))
    ch(v.tensor_tensor(e, e, d, ALU.mult))
    ch(v.tensor_scalar(e, e, -0.5, 1.5, ALU.mult, ALU.add))
    ch(v.tensor_tensor(y, y, e, ALU.mult))


def hops(c, tag, h, x0, keep, teleport, pairs, tail, norm=None, bias=None, out=None):
    nc, sem, at = c["nc"], c["sem"], c["at"]
    u, uf, xa, clo, cf, cl = (h[n] for n in ("u", "uf", "xa", "clo", "cf", "cl"))
    NG = T // G
    with ExitStack() as st:
        ps = st.enter_context(nc.psum_tensor(f"{tag}_ps", [128, HB, BANK], F32))
        s_ch, s_pre, s_prehi, s_b = (sem(f"{tag}_{n}") for n in ("ch", "pre", "prehi", "b"))
        s_pe, s_clo, s_w, s_uf, s_hi, s_u = (sem(f"{tag}_{n}") for n in ("pe", "clo", "w", "uf", "hi", "u"))
        s_out, s_stored = sem(f"{tag}_out"), sem(f"{tag}_stored")
        rn = RowNorm(c, st, f"{tag}_n", norm, u[tail % 2][:, 0:G, :].bitcast(F32)) if norm is not None else None
        b_sb = st.enter_context(nc.sbuf_tensor(f"{tag}_bias", [P, F], F32)) if bias else None

        def program(eng, one):
            if pairs:
                with eng.Fori(0, pairs) as i:
                    for hop in range(2):
                        for t in range(T):
                            one(hop, t, i * (2 * T) + (hop * T + t + 1), False)
            for hop in range(tail):
                for t in range(T):
                    one(hop, t, (2 * pairs + hop) * T + t + 1, hop == tail - 1)

        with nc.Block() as block:
            @block.gpsimd
            def _(pool):
                pool.sem_inc(s_w, HB)

            @block.sync
            def _(sp):
                if bias:
                    sp.dma_start(b_sb[:, :], row_vector(c, bias, P)).then_inc(s_b, 16)
                if out is not None:
                    for g in range(NG):
                        sp.wait_ge(s_out, g + 1)
                        sp.dma_start(node_view(out)[:, g * G:(g + 1) * G, :], norm[:, g * G:(g + 1) * G, :]).then_inc(s_stored, 16)
                    sp.wait_ge(s_stored, 16 * NG)

            @block.tensor
            def _(pe):
                def one(hop, t, n, last_hop):
                    pe.wait_ge(s_w, n)
                    for k in range(T):
                        if t == 0:
                            pe.wait_ge(s_u, n + k)
                        last = pe.matmul(ps[:, t % HB, 0:2 * F], at[:, k, t * P:t * P + 128], u[hop][:, k, :],
                                         start=(k == 0), stop=(k == T - 1))
                    last.then_inc(s_pe, 1)
                program(pe, one)

            @block.scalar
            def _(act):
                for g in range(NG):
                    gs = slice(g * G, (g + 1) * G)
                    act.wait_ge(s_pre, g + 1)
                    act.activation(u[0][:, gs, 0:F], uf[:, gs, :], ACT.Copy, scale=1.0 / LO).then_inc(s_prehi, 1)
                    act.activation(xa[:, gs, :], uf[:, gs, :], ACT.Copy, scale=teleport).then_inc(s_prehi, 1)

                def one(hop, t, n, last_hop):
                    b = t % HB
                    act.wait_ge(s_pe, n)
                    act.wait_ge(s_w, n)
                    act.activation(clo[:, b, :], ps[0:P, b, F:2 * F], ACT.Copy, scale=cl[:, t:t + 1]).then_inc(s_clo, 1)
                    if not last_hop:
                        act.wait_ge(s_uf, n)
                        act.activation(u[(hop + 1) % 2][:, t, 0:F], uf[:, t, :], ACT.Copy, scale=1.0 / LO).then_inc(s_hi, 1)
                    elif rn and t % G == G - 1:
                        rn.scalar(act, t // G)
                program(act, one)

            @block.vector
            def _(v):
                ch = Chain(v, s_ch)
                dinv = c["dinv"]
                ch(v.scalar_tensor_tensor(cf[:, :], dinv[:, :], LO * keep, dinv[:, :], ALU.mult, ALU.mult))
                ch(v.tensor_scalar(cl[:, :], cf[:, :], 1.0 / LO, None, ALU.mult))
                for g in range(NG):
                    gs = slice(g * G, (g + 1) * G)
                    v.tensor_tensor(uf[:, gs, :], x0[:, gs, :], bc(c["dinv_lo"][:, gs], F), ALU.mult).then_inc(s_pre, 1)
                for g in range(NG):
                    gs = slice(g * G, (g + 1) * G)
                    v.wait_ge(s_prehi, 2 * g + 1)
                    v.scalar_tensor_tensor(u[0][:, gs, F:2 * F], u[0][:, gs, 0:F], -LO, uf[:, gs, :],
                                           ALU.mult, ALU.add).then_inc(s_u, G)
                v.wait_ge(s_prehi, 2 * NG)
                if bias:
                    v.wait_ge(s_b, 16)

                def finish(g):
                    gs = slice(g * G, (g + 1) * G)
                    ch(v.tensor_tensor(uf[:, gs, :], uf[:, gs, :], bc(c["dsqrt"][:, gs], F), ALU.mult))
                    if bias:
                        ch(v.tensor_tensor(uf[:, gs, :], uf[:, gs, :], b_sb[:, :].unsqueeze(1).to_broadcast([P, G, F]), ALU.add))
                    if rn:
                        rn.vector(v, ch, g, uf[:, gs, :]).then_inc(s_out, 1)

                def one(hop, t, n, last_hop):
                    b = t % HB
                    v.wait_ge(s_clo, n)
                    v.scalar_tensor_tensor(uf[:, t, :], ps[0:P, b, 0:F], cf[:, t:t + 1], clo[:, b, :],
                                           ALU.mult, ALU.add).then_inc(s_w, 1)
                    v.wait_ge(s_w, n + HB)
                    v.tensor_tensor(uf[:, t, :], uf[:, t, :], xa[:, t, :], ALU.add).then_inc(s_uf, 1)
                    if not last_hop:
                        v.wait_ge(s_hi, n)
                        v.scalar_tensor_tensor(u[(hop + 1) % 2][:, t, F:2 * F], u[(hop + 1) % 2][:, t, 0:F], -LO,
                                               uf[:, t, :], ALU.mult, ALU.add).then_inc(s_u, 1)
                    elif t % G == G - 1:
                        v.wait_ge(s_uf, n)
                        finish(t // G)
                program(v, one)


def node_product(c, tag, xs, w1, w2=None, bias=None, hs=None, graph_norm=False):
    nc, sem, ident = c["nc"], c["sem"], c["ident"]
    m = 2 * F if w2 else F
    per = 2 if w2 else G
    turns = [range(i, min(i + BLK, T)) for i in range(0, T, BLK)]
    batches = [range(i, min(i + per, T)) for i in range(0, T, per)]
    kk = F + 1 if w2 else F
    with ExitStack() as st:
        def sb(name, shape, dt=F32):
            return st.enter_context(nc.sbuf_tensor(f"{tag}_{name}", shape, dt))
        wc = sb("w", [kk, m])
        xt = sb("xt", [kk, N]) if w2 else hs["wide"][0:F, :]
        y = sb("y", [P, T, 2 * F], F16) if w2 else hs["uf"]
        root = sb("root", [P, T, F]) if w2 else None
        par = sb("par", [F, 3]) if graph_norm else None
        part = sb("part", [F, 2 * len(turns)]) if graph_norm else None
        col = sb("col", [F, 8]) if graph_norm else None
        junk = hs["u"][0] if graph_norm else None
        pt = st.enter_context(nc.psum_tensor(f"{tag}_pt", [128, 3, BANK], F32))
        py = st.enter_context(nc.psum_tensor(f"{tag}_py", [128, 4, BANK], F32))
        s_w, s_scaled, s_t, s_c, s_y, s_hi, s_o, s_st, s_ch, s_n, s_m = (
            sem(f"{tag}_{n}") for n in ("w", "scaled", "t", "c", "y", "hi", "o", "st", "ch", "n", "m"))
        n_w = 16 * (1 + 2 * bool(w2) + 3 * graph_norm)
        NT, NB = len(turns), len(batches)

        def of(r, width):
            b = r.start // per
            return py[0:P, b % 4, 0:len(r) * m].rearrange("p (t f) -> p t f", f=m)[:, :, width]

        with nc.Block() as block:
            @block.sync
            def _(sp):
                sp.dma_start(wc[0:F, 0:F], c["w"][w1]).then_inc(s_w, 16)
                if graph_norm:
                    with nc.allow_non_contiguous_dma(reason="vectors of F values, one to a partition"):
                        for i, name in enumerate(("gn_weight", "gn_bias", "gn_scale")):
                            sp.dma_start(par[:, i:i + 1], c["w"][name].rearrange("(f o) -> f o", o=1)).then_inc(s_w, 16)
                if w2:
                    sp.dma_start(wc[0:F, F:m], c["w"][w2]).then_inc(s_w, 16)
                    sp.dma_start(wc[F:kk, F:m], c["w"][bias].rearrange("(o f) -> o f", o=1)).then_inc(s_w, 16)
                    yv, rv = node_view(c["y_d"]), node_view(c["root_d"])
                    cuts = [0, 8, 16, 24, T]
                    for a, b in zip(cuts, cuts[1:]):
                        sp.wait_ge(s_o, -(-b // per))
                        sp.dma_start(yv[:, a:b, :], y[:, a:b, :]).then_inc(s_st, 16)
                    sp.dma_start(rv, root[:, :, :]).then_inc(s_st, 16)
                    sp.wait_ge(s_st, 16 * len(cuts))

            @block.tensor
            def _(pe):
                def turn(i):
                    if i >= 3:
                        pe.wait_ge(s_c, i - 2)
                    for t in turns[i]:
                        last = pe.transpose(pt[0:F, i % 3, (t % BLK) * P:(t % BLK + 1) * P], xs[:, t, :], ident[0:P, 0:P])
                    last.then_inc(s_t, 1)

                for i in range(NT if graph_norm else 2):
                    turn(i)
                pe.wait_ge(s_w, n_w)
                if w2:
                    pe.wait_ge(s_scaled, 3)
                if graph_norm:
                    pe.wait_ge(s_n, NT + 1)
                done = NT if graph_norm else 2
                for b, r in enumerate(batches):
                    while done < NT and r.stop > (done - 1) * BLK:
                        turn(done)
                        done += 1
                    if not graph_norm:
                        pe.wait_ge(s_c, (r.stop - 1) // BLK + 1)
                    if b >= 4:
                        pe.wait_ge(s_o, b - 3)
                    for j, t in enumerate(r):
                        last = pe.matmul(py[0:P, b % 4, j * m:(j + 1) * m], xt[:, t * P:(t + 1) * P], wc[:, :],
                                         start=True, stop=True)
                    last.then_inc(s_y, 1)

            @block.scalar
            def _(act):
                def copy(i):
                    r = turns[i]
                    act.wait_ge(s_t, i + 1)
                    a = dict(accum_out=part[:, i:i + 1]) if graph_norm else {}
                    act.activation(xt[0:F, r.start * P:r.stop * P], pt[0:F, i % 3, 0:len(r) * P], ACT.Copy, **a).then_inc(s_c, 1)

                if graph_norm:
                    for i in range(NT):
                        copy(i)
                    act.wait_ge(s_m, 1)
                    for i, r in enumerate(turns):
                        act.activation(junk[0:F, :, :].rearrange("p t f -> p (t f)")[:, r.start * P:r.stop * P],
                                       xt[0:F, r.start * P:r.stop * P], ACT.Square, bias=col[:, 0:1],
                                       accum_out=part[:, NT + i:NT + i + 1]).then_inc(s_n, 1)
                    act.wait_ge(s_m, 2)
                    act.activation(col[:, 2:3], col[:, 1:2], ACT.Sqrt).then_inc(s_m, 1)
                    act.wait_ge(s_m, 4)
                    act.activation(xt[0:F, :], xt[0:F, :], ACT.Relu, bias=col[:, 5:6], scale=col[:, 4:5]).then_inc(s_n, 1)
                elif not w2:
                    for i in range(NT):
                        copy(i)
                if w2:
                    done = 0
                    for b, r in enumerate(batches):
                        while done < NT and r.stop + 2 * per > done * BLK:
                            copy(done)
                            done += 1
                        act.wait_ge(s_y, b + 1)
                        act.activation(y[:, r.start:r.stop, 0:F], of(r, slice(0, F)), ACT.Copy, scale=1.0 / LO).then_inc(s_hi, 1)

            @block.gpsimd
            def _(pool):
                if w2:
                    pool.memset(xt[F:kk, :], 1.0).then_inc(s_scaled, 1)
                    pool.memset(wc[F:kk, 0:F], 0.0).then_inc(s_scaled, 1)

            @block.vector
            def _(v):
                ch = Chain(v, s_ch)
                if w2:
                    v.wait_ge(s_w, n_w)
                    v.tensor_scalar(wc[0:F, 0:F], wc[0:F, 0:F], LO, None, ALU.mult).then_inc(s_scaled, 1)
                if graph_norm:
                    v.wait_ge(s_w, n_w)
                    v.wait_ge(s_c, NT)
                    ch(v.reduce_sum(col[:, 1:2], part[:, 0:NT], X_AXIS))
                    v.scalar_tensor_tensor(col[:, 0:1], col[:, 1:2], -1.0 / N, par[:, 2:3], ALU.mult, ALU.mult).then_inc(s_m, 1)
                    v.wait_ge(s_m, 1)
                    v.wait_ge(s_n, NT)
                    ch(v.reduce_sum(col[:, 1:2], part[:, NT:2 * NT], X_AXIS))
                    ch(v.tensor_scalar(col[:, 1:2], col[:, 1:2], 1.0 / N, EPS, ALU.mult, ALU.add))
                    v.sem_inc(s_m, 1)
                    v.wait_ge(s_m, 3)
                    ch(v.reciprocal(col[:, 3:4], col[:, 2:3]))
                    newton(v, ch, col[:, 3:4], col[:, 6:7], col[:, 1:2])
                    ch(v.tensor_tensor(col[:, 4:5], col[:, 3:4], par[:, 0:1], ALU.mult))
                    v.scalar_tensor_tensor(col[:, 5:6], col[:, 0:1], col[:, 4:5], par[:, 1:2], ALU.mult, ALU.add).then_inc(s_m, 1)
                for b, r in enumerate(batches):
                    if w2:
                        v.wait_ge(s_hi, b + 1)
                        v.scalar_tensor_tensor(y[:, r.start:r.stop, F:m], y[:, r.start:r.stop, 0:F], -LO, of(r, slice(0, F)),
                                               ALU.mult, ALU.add)
                        v.tensor_copy(root[:, r.start:r.stop, :], of(r, slice(F, m))).then_inc(s_o, 1)
                    else:
                        v.wait_ge(s_y, b + 1)
                        v.tensor_copy(y[:, r.start:r.stop, :], of(r, slice(0, F))).then_inc(s_o, 1)


def edge_conv(c, tag, src_cols, ea_t, w_edge):
    nc, ident, ident16 = c["nc"], c["ident"], c["ident16"]
    sems = []

    def sem(name):
        sems.append(nc.alloc_semaphore(name=name))
        return sems[-1]

    n_it = C // (G * G)
    slot = [q % 2 for q in range(G)]
    ago = [1, 3] + [2] * (G - 2)
    with ExitStack() as st:
        def sb(name, shape, dt):
            return st.enter_context(nc.sbuf_tensor(f"{tag}_{name}", shape, dt))
        gat = sb("gathered", [P, G, G, 2 * F], F16)
        idx_all = sb("idx_all", [P, C + G * G], I32)
        idx = sb("idx", [P, G, G], I32)
        comb = sb("scan_and_attr", [128, G, GE], F32)
        mk = sb("mask", [F, G, GE], BF16)
        back = sb("back", [P, G, G * F], F32)
        we = sb("we", [128, F], F32)
        msg = st.enter_context(nc.psum_tensor(f"{tag}_msg", [128, 2, 2, BANK], F32))
        tr = st.enter_context(nc.psum_tensor(f"{tag}_tr", [128, 2, BANK], F32))
        s_w, s_init, s_idx, s_msg, s_scan, s_half, s_tr, s_back, s_gate = (
            sem(f"{tag}_{n}") for n in ("w", "init", "idx", "msg", "scan", "half", "tr", "back", "gate"))
        s_gat, s_ea, s_mk, s_st = ([sem(f"{tag}_{n}{q}") for q in range(G)] for n in ("gat", "ea", "mk", "st"))
        scan_v = c["scan_d"].rearrange("(g j p) f -> g p j f", j=G, p=P)

        with nc.Block() as block:
            @block.sync
            def _(sp):
                sp.dma_start(idx_all[:, 0:C], src_cols).then_inc(s_w, 16)
                sp.dma_start(we[F:128, :], c["w"][w_edge]).then_inc(s_w, 16)
                with sp.Fori(0, n_it) as i:
                    for q in range(G):
                        n = i * G + q
                        sp.wait_ge(s_msg, n + 1)
                        sp.sem_inc(s_gate, 1)
                        sp.dma_start(comb[F:128, q, :], ea_t[:, bass.ds(n * GE, GE)]).then_inc(s_ea[q], 16)
                        sp.wait_ge(s_scan, n + 1)
                        sp.sem_inc(s_gate, 1)
                        sp.dma_start(mk[:, q, :], c["mask_d"][:, bass.ds(n * GE, GE)].to_broadcast([F, GE])).then_inc(s_mk[q], 16)

            @block.gpsimd
            def _(pool):
                for s in (s_msg, s_scan, s_tr, s_back):
                    pool.sem_inc(s, G)
                for s in s_st:
                    pool.sem_inc(s, 16)
                with pool.Fori(0, n_it) as i:
                    for q in range(G):
                        n = i * G + q
                        pool.wait_ge(s_msg, n + 1)
                        pool.wait_ge(s_idx, n + 1)
                        pool.sem_inc(s_gate, 1)
                        for j in range(G):
                            pool.indirect_dma_start(
                                out=gat[:, q, j, :], out_offset=None, in_=c["y_d"],
                                in_offset=bass.IndirectOffsetOnAxis(ap=idx[:, q, j:j + 1], axis=0),
                            ).then_inc(s_gat[q], 16)

            @block.tensor
            def _(pe):
                def messages(i, q):
                    n = i * G + q
                    pe.wait_ge(s_scan, n + (G + 1 - ago[q]))
                    pe.wait_ge(s_ea[q], 16 * i + 16)
                    pe.wait_ge(s_gat[q], 16 * G * i + 16 * G)
                    for j in range(G):
                        b, o = divmod(j, BLK)
                        at = msg[0:F, slot[q], b, o * P:(o + 1) * P]
                        pe.matmul(at, gat[:, q, j, 0:F], ident16[:, 0, :], start=True, stop=False)
                        pe.matmul(at, gat[:, q, j, F:2 * F], ident16[:, 1, :], start=False, stop=False)
                        last = pe.matmul(at, we[F:128, :], comb[F:128, q, j * P:(j + 1) * P], start=False, stop=True)
                    last.then_inc(s_msg, 1)

                def turn_back(i, q):
                    n = i * G + q
                    pe.wait_ge(s_back, n + (G + 1 - ago[q]))
                    pe.wait_ge(s_scan, n + (G + 1))
                    for j in range(G):
                        last = pe.transpose(tr[0:P, slot[q], j * F:(j + 1) * F], comb[0:F, q, j * P:(j + 1) * P],
                                            ident[0:F, 0:F])
                    last.then_inc(s_tr, 1)

                pe.wait_ge(s_w, 32)
                with pe.Fori(0, n_it) as i:
                    messages(i, 0)
                    for q in range(1, G):
                        messages(i, q)
                        turn_back(i, q - 1)
                    turn_back(i, G - 1)

            @block.vector
            def _(v):
                v.memset(idx_all[:, C:C + G * G], 0)
                v.memset(comb[0:F, G - 1, GE - 1:GE], 0.0).then_inc(s_init, 1)
                v.wait_ge(s_init, 1)
                v.wait_ge(s_w, 32)
                for q in range(G):
                    v.tensor_copy(idx[:, q, :], idx_all[:, q * G:(q + 1) * G]).then_inc(s_idx, 1)
                with v.Fori(0, n_it) as i:
                    for q in range(G):
                        n = i * G + q
                        v.wait_ge(s_mk[q], 16 * i + 16)
                        v.wait_ge(s_tr, n + 1)
                        v.wait_ge(s_scan, n + G)
                        v.wait_ge(s_msg, n + (G + 1))
                        v.tensor_tensor_scan(comb[0:F, q, 0:GE - P], mk[:, q, 0:GE - P], msg[0:F, slot[q], 0, 0:GE - P],
                                             comb[0:F, (q - 1) % G, GE - 1:GE], ALU.add, ALU.max).then_inc(s_half, 1)
                        v.wait_ge(s_half, n + 1)
                        v.tensor_tensor_scan(comb[0:F, q, GE - P:GE], mk[:, q, GE - P:GE], msg[0:F, slot[q], 1, 0:P],
                                             comb[0:F, q, GE - P - 1:GE - P], ALU.add, ALU.max).then_inc(s_scan, 1)
                        v.tensor_copy(idx[:, q, :], idx_all[:, bass.ds((n + G) * G, G)]).then_inc(s_idx, 1)

            @block.scalar
            def _(act):
                with act.Fori(0, n_it) as i:
                    for q in range(G):
                        n = i * G + q
                        act.wait_ge(s_st[q], 16 * i + 16)
                        act.wait_ge(s_tr, n + (G + 1))
                        act.copy(back[:, q, :], tr[0:P, slot[q], 0:G * F]).then_inc(s_back, 1)
                        act.wait_ge(s_back, n + (G + 1))
                        act.dma_start(scan_v[bass.ds(n, 1), :, :, :].rearrange("o p j f -> (o p) j f"),
                                      back[:, q, :].rearrange("p (j f) -> p j f", f=F)).then_inc(s_st[q], 16)
                for q in range(G):
                    act.wait_ge(s_st[q], 16 * n_it + 16)
    nc.clear_and_free_semaphores(sems)
    nc.all_engine_barrier()


def conv_result(c, tag, res, norm):
    nc, sem = c["nc"], c["sem"]
    with ExitStack() as st:
        root = st.enter_context(nc.sbuf_tensor(f"{tag}_root", [P, T, F], F32))
        s_g = [sem(f"{tag}_g{g}") for g in range(T // G)]
        s_r, s_ch = sem(f"{tag}_r"), sem(f"{tag}_ch")
        rn = None
        if norm is not None:
            sq = st.enter_context(nc.sbuf_tensor(f"{tag}_sq", [P, G, F], F32))
            rn = RowNorm(c, st, f"{tag}_n", norm, sq[:, :, :])
        with nc.Block() as block:
            @block.gpsimd
            def _(pool):
                for t in range(T):
                    pool.indirect_dma_start(out=res[:, t, :], out_offset=None, in_=c["scan_d"],
                                            in_offset=bass.IndirectOffsetOnAxis(ap=c["end_idx"][:, t:t + 1], axis=0),
                                            ).then_inc(s_g[t // G], 16)

            @block.sync
            def _(sp):
                sp.dma_start(root[:, :, :], node_view(c["root_d"])).then_inc(s_r, 16)

            @block.scalar
            def _(act):
                if rn:
                    for g in range(T // G):
                        rn.scalar(act, g)

            @block.vector
            def _(v):
                ch = Chain(v, s_ch)
                v.wait_ge(s_r, 16)
                for g in range(T // G):
                    gs = slice(g * G, (g + 1) * G)
                    v.wait_ge(s_g[g], 16 * G)
                    ch(v.tensor_tensor(res[:, gs, :], res[:, gs, :], bc(c["has_in"][:, gs], F), ALU.mult))
                    ch(v.tensor_tensor(root[:, gs, :], root[:, gs, :], res[:, gs, :], ALU.add))
                    ch(v.scalar_tensor_tensor(res[:, gs, :], root[:, gs, :], 0.01, root[:, gs, :], ALU.mult, ALU.max))
                    if rn:
                        rn.vector(v, ch, g, res[:, gs, :])


_WEIGHTS = {"W1_msg": "L1_gnn_W1_msg", "W1_edge": "L1_gnn_W1_edge", "W1_root": "L1_gnn_W1_root", "b1": "L1_gnn_b1",
            "W2_msg": "L1_gnn_W2_msg", "W2_edge": "L1_gnn_W2_edge", "W2_root": "L1_gnn_W2_root", "b2": "L1_gnn_b2",
            "g_W1": "L3_gnn_W1", "g_b1": "L3_gnn_b1", "gn_weight": "L3_gnn_gn_weight", "gn_bias": "L3_gnn_gn_bias",
            "gn_scale": "L3_gnn_gn_mean_scale", "g_W2": "L3_gnn_W2", "g_b2": "L3_gnn_b2"}


def kernel(**inputs):
    import numpy as np
    import concourse.bacc as bacc
    from concourse.bass_utils import run_bass_kernel_spmd

    nc = bacc.Bacc("TRN2", target_bir_lowering=False, num_devices=1)
    src = np.asarray(inputs["src"])
    arrays = {
        "x": np.ascontiguousarray(inputs["x"]),
        "src": np.ascontiguousarray(src),
        "dst": np.ascontiguousarray(inputs["dst"]),
        "src_cols": np.ascontiguousarray(src.reshape(C, P).T),
        "ea_t": np.ascontiguousarray(np.asarray(inputs["edge_attr_32"]).T),
    }
    for short, name in _WEIGHTS.items():
        arrays["w_" + short] = np.ascontiguousarray(inputs[name])
    aps = {n: nc.dram_tensor("in_" + n, a.shape, mybir.dt.from_np(a.dtype), kind="ExternalInput").ap()
           for n, a in arrays.items()}
    out = nc.dram_tensor("out_x", (N, F), F32, kind="ExternalOutput").ap()
    build(nc, aps["x"], aps["src"], aps["dst"], aps["src_cols"], aps["ea_t"], {n: aps["w_" + n] for n in _WEIGHTS}, out)
    r = run_bass_kernel_spmd(nc, [{"in_" + n: a for n, a in arrays.items()}], core_ids=[0])
    return r.results[0]["out_x"]
```

```python
import concourse.bass as bass
from concourse import mybir
from contextlib import ExitStack, contextmanager

F32 = mybir.dt.float32
F16 = mybir.dt.float16
BF16 = mybir.dt.bfloat16
I32 = mybir.dt.int32
ALU = mybir.AluOpType
ACT = mybir.ActivationFunctionType
X_AXIS = mybir.AxisListType.X

N, F, E = 3125, 96, 53125
P = 125
T = N // P
C = E // P
SRC_MID = N // 2
YS = 16.0
LO = 2048.0
NEG = -3.0e38
MAGIC = 1.5 * 2.0 ** 23
K = 128
W = 25
S = P // W
NW = N // W
WK = -(-E // (NW * K))
WIN = WK * K
HOTW = T * W + 1
ATW = N + 3
BLK = 4
BANK = 512
G = 5
GE = G * P
HB = 5
EPS = 1e-5


class Chain:

    def __init__(self, eng, sem):
        self.eng, self.sem, self.n = eng, sem, 0

    def __call__(self, ins):
        self.n += 1
        ins.then_inc(self.sem, 1)
        self.eng.wait_ge(self.sem, self.n)


@contextmanager
def phase_semaphores(nc):
    made = []

    def sem(name):
        made.append(nc.alloc_semaphore(name=name))
        return made[-1]

    yield sem
    nc.clear_and_free_semaphores(made)
    nc.all_engine_barrier()


def build(nc, x, src, dst, src_cols, ea_t, w, out):
    top = ExitStack()
    with top:
        def keep(name, shape, dt):
            return top.enter_context(nc.sbuf_tensor(name, shape, dt))

        def sem(name):
            return top.enter_context(nc.semaphore(name))

        at = keep("counts", [P, T, ATW], F16)
        ident = keep("ident", [128, 128], F32)
        ident16 = keep("ident16", [P, P], F16)
        dinv = keep("dinv", [P, T], F32)
        dinv_lo = keep("dinv_lo", [P, T], F32)
        dsqrt = keep("dsqrt", [P, T], F32)
        has_in = keep("has_in", [P, T], F32)
        end_idx = keep("end_idx", [P, T], I32)
        start_f = keep("start_f", [1, T], F32)

        ev_d = nc.dram_tensor("edge_values", (E + WIN, 3), F32).ap()
        mask_d = nc.dram_tensor("segment_mask", (1, E), BF16).ap()
        src_d = nc.dram_tensor("sources", (1, E), F16).ap()
        y_d = nc.dram_tensor("messages", (N, 2 * F), F16).ap()
        root_d = nc.dram_tensor("root_parked", (P, T, F), F32).ap()
        scan_d = nc.dram_tensor("running_max", (E, F), F32).ap()
        ctx = dict(nc=nc, sem=sem, at=at, ident=ident, ident16=ident16, dinv=dinv, dinv_lo=dinv_lo, dsqrt=dsqrt,
                   has_in=has_in, end_idx=end_idx, start_f=start_f, ev_d=ev_d, mask_d=mask_d, src_d=src_d, y_d=y_d,
                   root_d=root_d, scan_d=scan_d, w=w, src_cols=src_cols)
        xs = keep("x_state", [P, T, F], F32)
        ctx["idx_all"] = keep("idx_all", [P, C + G * G], I32)
        ctx["deg"] = keep("deg", [P, T], F32)
        build_counts(ctx, src, dst, xs, x)
        degrees(ctx)
        with ExitStack() as st:
            hs = hop_state(ctx, st, "l0")
            hops(ctx, "l0", hs, xs, 1.0, 0.0, 0, 2, norm=xs)
        with ExitStack() as st:
            y1 = st.enter_context(nc.sbuf_tensor("y1", [P, T, 2 * F], F16))
            node_product(ctx, "c1w", xs, "W1_msg", "W1_root", "b1", y16=y1)
            edge_conv(ctx, "c1", ea_t, "W1_edge", y1)
        with ExitStack() as st:
            y2 = st.enter_context(nc.sbuf_tensor("y2", [P, T, 2 * F], F16))
            with ExitStack() as s2:
                c1 = s2.enter_context(nc.sbuf_tensor("c1", [P, T, F], F32))
                conv = ConvResult(ctx, s2, "c1r", c1)
                node_product(ctx, "c2w", c1, "W2_msg", "W2_root", "b2", y16=y2, conv=conv)
            edge_conv(ctx, "c2", ea_t, "W2_edge", y2)
        with ExitStack() as st:
            c2 = st.enter_context(nc.sbuf_tensor("c2", [P, T, F], F32))
            conv_result(ctx, "c2r", c2, xs)
        with ExitStack() as st:
            hs = hop_state(ctx, st, "l2")
            h = hs["uf"]
            hops(ctx, "l2", hs, xs, 0.9, 0.1, 7, 2, norm=xs)
            node_product(ctx, "g1w", xs, "g_W1", hs=hs)
            hops(ctx, "g1", hs, h, 1.0, 0.0, 0, 1, bias="g_b1")
            node_product(ctx, "g2w", h, "g_W2", hs=hs, graph_norm=True)
            hops(ctx, "g2", hs, h, 1.0, 0.0, 0, 1, bias="g_b2", norm=xs, out=out)


def bc(ap, n):
    return ap.unsqueeze(2).to_broadcast([ap.shape[0], ap.shape[1], n])


def node_view(dram):
    return dram.rearrange("(t p) f -> p t f", p=P)


def build_counts(c, src, dst, xs, x):
    nc = c["nc"]
    with ExitStack() as st:
        def sb(name, shape, dt):
            return st.enter_context(nc.sbuf_tensor(name, shape, dt))
        tab = dict(iota=sb("iota", [K, HOTW], F16), wbase=sb("wbase", [K, NW], F32), start_i=sb("start_i", [1, NW], I32),
                   start=sb("start", [1, NW + 1], F32), further=sb("further", [1, 3], I32))
        with ExitStack() as s1:
            edge_values(c, s1, src, dst, tab, xs, x)
        with ExitStack() as s1:
            table_rounds(c, s1, s1.enter_context(phase_semaphores(nc)), tab)


def edge_values(c, st, src, dst, tab, xs, x):
    nc, sem, ident = c["nc"], c["sem"], c["ident"]

    def sb(name, shape, dt):
        return st.enter_context(nc.sbuf_tensor(name, shape, dt))

    di, si, pv = sb("di", [P, C], I32), sb("si", [P, C], I32), sb("pv", [P, 1], I32)
    ev = sb("ev", [P, C, 3], F32)
    dstf, srcf, pvf = sb("dstf", [P, C], F32), sb("srcf", [P, C], F32), sb("pvf", [P, 1], F32)
    tile16, sub16 = sb("tile16", [P, C], F16), sb("sub16", [P, C], F16)
    tmp, neq = sb("tmp", [P, C], F32), sb("neq", [P, C], F32)
    mask, src16 = sb("mask", [P, C], BF16), sb("src16", [P, C], F16)
    pidx, fidx = sb("pidx", [K, 1], F32), sb("fidx", [K, K], F32)
    i25 = sb("i25", [P, T], F16)
    flat = c["at"][:, :, :].rearrange("p t d -> p (t d)")
    hot_t = flat[:, 0:C * T].rearrange("p (c t) -> p c t", t=T)
    hot_s = flat[:, C * T + 1:C * (T + S) + 1].rearrange("p (c s) -> p c s", s=S)
    same = sb("same", [P, G, S], F32)
    part, pair = sb("part", [P, G], F32), sb("pair", [P, G, S], F32)
    blk, tl, bin_no = sb("blk", [P, 1], F32), sb("tl", [P, 1], F32), sb("bin_no", [P, S], F32)
    before = sb("before", [P, S, NW], F32)
    hist = sb("hist", [P, S], F32)
    pad = sb("pad", [K, 3 * WK], F32)
    count, most = sb("count", [1, NW], F32), sb("most", [1, 1], F32)
    ps = st.enter_context(nc.psum_tensor("hist_ps", [128, BANK], F32))
    ps2 = st.enter_context(nc.psum_tensor("start_ps", [128, BANK], F32))
    s_dst, s_src, s_prev, s_iota, s_ch = (sem(f"k_{n}") for n in ("dst", "src", "prev", "iota", "chain"))
    s_x, s_cols, s_ev, s_mask, s_hot, s_hist, s_part, s_start, s_store = (
        sem(f"k_{n}") for n in ("x", "cols", "ev", "mask", "hot", "hist", "part", "start", "store"))
    dst_v, src_v = (a.rearrange("(p c) -> p c", p=P) for a in (dst, src))
    ev_flat = c["ev_d"].rearrange("e a -> (e a)")

    with nc.Block() as block:
        @block.sync
        def _(sp):
            sp.dma_start(di[:, :], dst_v).then_inc(s_dst, 16)
            sp.dma_start(si[:, :], src_v).then_inc(s_src, 16)
            sp.dma_start(xs[:, :, :], node_view(x)).then_inc(s_x, 16)
            sp.dma_start(c["idx_all"][:, 0:C], c["src_cols"]).then_inc(s_cols, 16)
            sp.wait_ge(s_ev, 1)
            sp.dma_start(ev_flat[0:3 * E].rearrange("(p c) -> p c", p=P), ev[:, :, :].rearrange("p c a -> p (c a)")).then_inc(s_store, 16)
            sp.dma_start(ev_flat[3 * E:3 * (E + WIN)].rearrange("(p c) -> p c", p=K), pad[:, :]).then_inc(s_store, 16)
            sp.dma_start(c["src_d"].rearrange("o (p c) -> (o p) c", p=P), src16[:, :]).then_inc(s_store, 16)
            sp.wait_ge(s_mask, 1)
            sp.dma_start(c["mask_d"].rearrange("o (p c) -> (o p) c", p=P), mask[:, :]).then_inc(s_store, 16)
            sp.wait_ge(s_store, 64)
            sp.wait_ge(s_x, 16)
            sp.wait_ge(s_cols, 16)

        @block.scalar
        def _(act):
            act.wait_ge(s_iota, 1)
            with nc.allow_non_contiguous_dma(reason="the last dst of each partition, single values"):
                act.dma_start(pv[1:P, 0:1], dst_v[0:P - 1, C - 1:C]).then_inc(s_prev, 16)
            act.wait_ge(s_prev, 16)

        @block.gpsimd
        def _(pool):
            pool.memset(pv[:, :], -1).then_inc(s_iota, 1)
            pool.iota(i25[:, :], pattern=[[1, T]], base=0, channel_multiplier=0,
                      allow_small_or_imprecise_dtypes=True).then_inc(s_iota, 1)
            pool.iota(pidx[:, :], pattern=[[0, 1]], base=0, channel_multiplier=1,
                      allow_small_or_imprecise_dtypes=True).then_inc(s_iota, 1)
            pool.iota(fidx[:, :], pattern=[[1, K]], base=0, channel_multiplier=0,
                      allow_small_or_imprecise_dtypes=True).then_inc(s_iota, 1)
            pool.iota(tab["iota"][:, :], pattern=[[1, HOTW]], base=0, channel_multiplier=0,
                      allow_small_or_imprecise_dtypes=True).then_inc(s_iota, 1)
            pool.iota(tab["wbase"][:, :], pattern=[[W, NW]], base=0, channel_multiplier=0,
                      allow_small_or_imprecise_dtypes=True).then_inc(s_iota, 1)

        @block.vector
        def _(v):
            ch = Chain(v, s_ch)

            def tile_of(out, a, size):
                ch(v.tensor_scalar(out, a, float(size // 2), 1.0 / size, ALU.subtract, ALU.mult))
                ch(v.tensor_scalar(out, out, MAGIC, MAGIC, ALU.add, ALU.subtract))

            v.memset(pad[:, :], -1.0)
            v.memset(c["idx_all"][:, C:C + G * G], 0)
            v.memset(tab["start"][:, NW:NW + 1], float(E))
            v.wait_ge(s_iota, 4)
            v.tensor_scalar(ident[:, :], fidx[:, :], pidx[:, :], None, ALU.is_equal)
            tile_of(blk[:, :], pidx[0:P, :], T)
            ch(v.scalar_tensor_tensor(tl[:, :], blk[:, :], -float(T), pidx[0:P, :], ALU.mult, ALU.add))
            for b in range(G):
                v.tensor_scalar(same[:, b, :], blk[:, :].to_broadcast([P, S]), float(b), None, ALU.is_equal)
                v.tensor_scalar(bin_no[:, b:b + 1], tl[:, :], float(S), float(b), ALU.mult, ALU.add)
            ch(v.memset(part[:, :], 0.0))
            for b in range(S):
                v.tensor_scalar(before[:, b, :], fidx[0:P, 0:NW], bin_no[:, b:b + 1], None, ALU.is_gt)
            v.wait_ge(s_dst, 16)
            ch(v.tensor_copy(dstf[:, :], di[:, :]))
            tile_of(tmp[:, :], dstf[:, :], P)
            ch(v.tensor_copy(tile16[:, :], tmp[:, :]))
            v.tensor_tensor(hot_t[:, :, :], bc(tile16[:, :], T), i25[:, :].unsqueeze(1).to_broadcast([P, C, T]), ALU.is_equal)
            ch(v.scalar_tensor_tensor(tmp[:, :], tmp[:, :], -float(P), dstf[:, :], ALU.mult, ALU.add))
            tile_of(tmp[:, :], tmp[:, :], W)
            ch(v.tensor_copy(sub16[:, :], tmp[:, :]))
            v.tensor_tensor(hot_s[:, :, :], bc(sub16[:, :], S), i25[:, 0:S].unsqueeze(1).to_broadcast([P, C, S]),
                            ALU.is_equal).then_inc(s_hot, 1)
            v.wait_ge(s_src, 16)
            v.tensor_copy(ev[:, :, 2], dstf[:, :])
            ch(v.tensor_copy(srcf[:, :], si[:, :]))
            v.tensor_scalar(src16[:, :], srcf[:, :], float(SRC_MID), None, ALU.subtract)
            tile_of(tmp[:, :], srcf[:, :], P)
            v.scalar_tensor_tensor(ev[:, :, 1], tmp[:, :], -float(P), srcf[:, :], ALU.mult, ALU.add)
            v.scalar_tensor_tensor(ev[:, :, 0], tmp[:, :], float(W), dstf[:, :], ALU.mult, ALU.add).then_inc(s_ev, 1)
            v.wait_ge(s_hist, 1)
            ch(v.tensor_tensor(pair[:, :, :], ps[0:P, 0:G * S].rearrange("p (b s) -> p b s", s=S), same[:, :, :], ALU.mult))
            v.reduce_sum(hist[:, :], pair[:, :, :].rearrange("p b s -> p s b"), X_AXIS).then_inc(s_part, 1)
            v.wait_ge(s_start, 1)
            v.tensor_copy(tab["start_i"][:, :], ps2[0:1, 0:NW])
            ch(v.tensor_copy(tab["start"][:, 0:NW], ps2[0:1, 0:NW]))
            ch(v.tensor_tensor(count[:, :], tab["start"][:, 1:NW + 1], tab["start"][:, 0:NW], ALU.subtract))
            ch(v.reduce_max(most[:, :], count[:, :], X_AXIS))
            ch(v.tensor_scalar(most[:, :], most[:, :], 1.0 + (WIN - 1) / 2.0, 1.0 / WIN, ALU.subtract, ALU.mult))
            ch(v.tensor_scalar(most[:, :], most[:, :], MAGIC, MAGIC, ALU.add, ALU.subtract))
            v.tensor_scalar(count[:, 0:1], most[:, :], 1.0, None, ALU.max)
            v.tensor_scalar(count[:, 1:2], most[:, :], 1.0, float(NW - 1), ALU.min, ALU.mult)
            ch(v.tensor_scalar(count[:, 2:3], most[:, :], 1.0, float(T - 2), ALU.min, ALU.mult))
            ch(v.tensor_scalar(count[:, 1:3], count[:, 1:3], 1.0, None, ALU.add))
            v.tensor_copy(tab["further"][:, :], count[:, 0:3])
            v.tensor_copy(c["start_f"][:, :], ps2[0:1, 0:NW].rearrange("o (t s) -> o t s", s=S)[:, :, 0])
            v.wait_ge(s_prev, 16)
            ch(v.tensor_copy(pvf[:, :], pv[:, :]))
            v.tensor_tensor(neq[:, 1:C], dstf[:, 1:C], dstf[:, 0:C - 1], ALU.not_equal)
            ch(v.tensor_tensor(neq[:, 0:1], dstf[:, 0:1], pvf[:, :], ALU.not_equal))
            v.tensor_scalar(mask[:, :], neq[:, :], NEG, None, ALU.mult).then_inc(s_mask, 1)

        @block.tensor
        def _(pe):
            pe.wait_ge(s_hot, 1)
            for g in range(C // G):
                last = pe.matmul(ps[0:P, 0:G * S], hot_t[:, g * G:(g + 1) * G, :].rearrange("p c t -> p (c t)"),
                                 hot_s[:, g * G:(g + 1) * G, :].rearrange("p c s -> p (c s)"),
                                 start=(g == 0), stop=(g == C // G - 1))
            last.then_inc(s_hist, 1)
            pe.wait_ge(s_part, 1)
            for b in range(S):
                last = pe.matmul(ps2[0:1, 0:NW], hist[:, b:b + 1], before[:, b, :], start=(b == 0), stop=(b == S - 1))
            last.then_inc(s_start, 1)


def table_rounds(c, st, sem, tab):
    nc, at, iota, wbase, start_i = c["nc"], c["at"], tab["iota"], tab["wbase"], tab["start_i"]

    def sb(name, shape, dt):
        return st.enter_context(nc.sbuf_tensor(name, shape, dt))
    hot = sb("hot", [K, S, WK, HOTW], F16)
    low = sb("low_hot", [K, S, WK, 128], F16)
    win = sb("win", [K, NW, WK, 3], F32)
    key, lkey = sb("key", [K, S, WK], F32), sb("low_key", [K, S, WK], F32)
    key_n, far, out_by = (sb(n, [K, S, WK], F32) for n in ("key_next", "far", "out_by"))
    ones = sb("deg_ones", [P, 2], F16)
    ps = st.enter_context(nc.psum_tensor("count_ps", [128, 3, 2, BANK], F32))
    ps_deg = st.enter_context(nc.psum_tensor("deg_ps", [128, BANK], F32))
    s_gate, s_step, s_key, s_low, s_hot, s_bank, s_flush, s_one, s_deg = (
        sem(f"t_{n}") for n in ("gate", "step", "key", "low", "hot", "bank", "flush", "one", "deg"))
    s_win = [sem(f"t_win{q}") for q in range(S)]
    slot = [q % 3 for q in range(S)]
    ago = [2, 2, 3, 3, 3]
    FIRST = BLK * P
    POOL_WINDOW = 2
    STEPS = 5

    def pieces(w_slot):
        for b, (lo, hi) in enumerate(((0, FIRST // W), (FIRST // W, T))):
            yield slice(lo, hi), ps[0:P, w_slot, b, 0:(hi - lo) * W].rearrange("p (h d) -> p h d", d=W)

    def products(pe, w_slot, lows, hots):
        for k in range(WK):
            for b, (lo, hi) in enumerate(((0, FIRST), (FIRST, T * W))):
                last = pe.matmul(ps[:, w_slot, b, 0:hi - lo], lows[:, k, :], hots[:, k, lo:hi],
                                 start=(k == 0), stop=(k == WK - 1))
        return last

    def edges_from(first):
        return c["ev_d"][bass.ds(first, WIN), :].rearrange("(p k) a -> p (k a)", p=K)

    def key_steps(v, edges, base, k_out, l_out, tmp):
        yield (lambda: v.tensor_tensor(k_out, edges[0], base, ALU.subtract),
               lambda: v.tensor_tensor(tmp, edges[2], base, ALU.subtract))
        yield (lambda: v.tensor_scalar(l_out, tmp, float(W - 1), None, ALU.subtract),)
        yield (lambda: v.scalar_tensor_tensor(tmp, tmp, -1.0, l_out, ALU.mult, ALU.max),)
        yield (lambda: v.tensor_scalar(tmp, tmp, 0.0, 1.0, ALU.max, ALU.min),)
        yield (lambda: v.scalar_tensor_tensor(l_out, tmp, 128.0, edges[1], ALU.mult, ALU.add),)

    with nc.Block() as block:
        def load(eng, q, n):
            first = eng.value_load(start_i[0:1, bass.ds(n, 1)], min_val=0, max_val=E)
            eng.dma_start(win[:, bass.ds(n, 1), :, :].rearrange("p o k a -> p (o k a)"),
                          edges_from(first)).then_inc(s_win[q], 16)

        def load_next(eng, q, t):
            eng.wait_ge(s_win[q], 16 * t)
            eng.sem_inc(s_gate, 1)
            load(eng, q, t * S + q)

        @block.sync
        def _(sp):
            mine = [q for q in range(S) if q != POOL_WINDOW]
            for q in mine:
                load(sp, q, q)
            with sp.Fori(1, T) as t:
                for q in mine:
                    load_next(sp, q, t)

        @block.gpsimd
        def _(pool):
            pool.sem_inc(s_bank, S)
            pool.sem_inc(s_flush, S)
            load(pool, POOL_WINDOW, POOL_WINDOW)

            def tile(t, more):
                if more:
                    load_next(pool, POOL_WINDOW, t + 1)
                for q in range(S):
                    pool.wait_ge(s_bank, S * t + q + 1)
                    pool.wait_ge(s_key, t + 1)
                    pool.tensor_tensor(low[:, q, :, :], iota[:, 0:128].unsqueeze(1).to_broadcast([K, WK, 128]),
                                       bc(lkey[:, q, :], 128), ALU.subtract).then_inc(s_low, 1)

            with pool.Fori(0, T - 1) as t:
                tile(t, True)
            tile(T - 1, False)

        @block.vector
        def _(v):
            v.memset(at[:, :, N:ATW], 0.0)

            def steps_of(t):
                edges = [win[:, bass.ds(t * S, S), :, a] for a in range(3)]
                return key_steps(v, edges, bc(wbase[:, bass.ds(t * S, S)], WK), key_n[:, :, :], out_by[:, :, :], far[:, :, :])

            def step(now):
                for make in now:
                    last = make()
                last.then_inc(s_step, 1)

            def tile(t, more):
                v.wait_ge(s_step, STEPS * t + STEPS)
                v.wait_ge(s_low, S * t + 1)
                v.wait_ge(s_hot, S * t + 1)
                v.tensor_copy(lkey[:, :, :], out_by[:, :, :])
                v.tensor_copy(key[:, :, :], key_n[:, :, :]).then_inc(s_key, 1)
                v.wait_ge(s_key, t + 1)
                nxt = steps_of(t + 1) if more else None
                for q in range(S):
                    v.wait_ge(s_bank, S * t + q + 1)
                    for k in range(WK):
                        last = v.tensor_scalar(hot[:, q, k, :], iota[:, :], key[:, q, k:k + 1], None, ALU.is_equal)
                    v.wait_ge(s_low, S * t + q + 2)
                    v.tensor_scalar(low[:, q, :, :], low[:, q, :, :], 0.0, None, ALU.is_equal).then_inc(s_hot, 1)
                    if more:
                        if q == 0:
                            for r in range(S):
                                v.wait_ge(s_win[r], 16 * t + 32)
                        v.wait_ge(s_step, STEPS * (t + 1) + q)
                        step(next(nxt))

            v.sem_inc(s_low, 1)
            v.sem_inc(s_hot, 1)
            for r in range(S):
                v.wait_ge(s_win[r], 16)
            for i, now in enumerate(steps_of(0)):
                if i:
                    v.wait_ge(s_step, i)
                step(now)
            with v.Fori(0, T - 1) as t:
                tile(t, True)
            tile(T - 1, False)

        @block.tensor
        def _(pe):
            with pe.Fori(0, T) as t:
                for q in range(S):
                    n = t * S + q
                    pe.wait_ge(s_flush, n + (S + 1 - ago[q]))
                    pe.wait_ge(s_hot, n + 2)
                    products(pe, slot[q], low[:, q, :, :], hot[:, q, :, :]).then_inc(s_bank, 1)

        @block.scalar
        def _(act):
            with act.Fori(0, T) as t:
                for q in range(S):
                    n = t * S + q
                    act.wait_ge(s_bank, n + (S + 1))
                    for i, (tiles, counts) in enumerate(pieces(slot[q])):
                        last = act.copy(at[:, tiles, bass.ds(n * W, W)], counts)
                    last.then_inc(s_flush, 1)

    s_round, s_load, s_do, s_hot2, s_bank2, s_added, s_whole = (
        sem(f"r_{n}") for n in ("round", "load", "do", "hot", "bank", "added", "whole"))
    further, start = tab["further"], tab["start"]

    def rounds_and_windows(eng, on_round, on_window):
        n_round = eng.value_load(further[0:1, 0:1], min_val=1, max_val=E // WIN)
        n_window = eng.value_load(further[0:1, 1:2], min_val=1, max_val=NW)
        with eng.Fori(0, n_round) as r:
            on_round(r)
            with eng.Fori(0, n_window) as n:
                on_window(n, r * NW + n)

    with nc.Block() as block:
        @block.sync
        def _(sp):
            def on_round(r):
                sp.wait_ge(s_round, 2 * r + 2)
                sp.sem_inc(s_gate, 1)

            def on_window(n, m):
                sp.wait_ge(s_added, m + 1)
                sp.sem_inc(s_gate, 1)
                first = sp.value_load(start_i[0:1, bass.ds(n, 1)], min_val=0, max_val=E)
                sp.dma_start(win[:, 0, :, :].rearrange("p k a -> p (k a)"), edges_from(first)).then_inc(s_load, 16)
            rounds_and_windows(sp, on_round, on_window)

        @block.gpsimd
        def _(pool):
            pool.memset(ones[:, :], 1.0).then_inc(s_one, 1)
            pool.sem_inc(s_added, 1)

        @block.vector
        def _(v):
            def on_round(r):
                v.tensor_scalar(start[:, 0:NW], start[:, 0:NW], float(WIN), float(E), ALU.add, ALU.min).then_inc(s_round, 1)
                v.wait_ge(s_round, 2 * r + 1)
                v.tensor_copy(start_i[:, :], start[:, 0:NW]).then_inc(s_round, 1)

            def on_window(n, m):
                edges = [win[:, 0:1, :, a] for a in range(3)]
                base = bc(wbase[:, bass.ds(n, 1)], WK)
                v.wait_ge(s_load, 16 * m + 16)
                for i, now in enumerate(key_steps(v, edges, base, key[:, 0:1, :], lkey[:, 0:1, :], far[:, 0:1, :])):
                    for make in now:
                        last = make()
                    last.then_inc(s_do, 1)
                    v.wait_ge(s_do, m * STEPS + (i + 1))
                for k in range(WK):
                    v.tensor_scalar(low[:, 0, k, :], iota[:, 0:128], lkey[:, 0, k:k + 1], None, ALU.is_equal)
                    last = v.tensor_scalar(hot[:, 0, k, :], iota[:, :], key[:, 0, k:k + 1], None, ALU.is_equal)
                last.then_inc(s_hot2, 1)
                v.wait_ge(s_bank2, m + 1)
                for tiles, counts in pieces(0):
                    to = at[:, tiles, bass.ds(n * W, W)]
                    last = v.tensor_tensor(to, to, counts, ALU.add)
                last.then_inc(s_added, 1)
                v.wait_ge(s_added, m + 2)
            rounds_and_windows(v, on_round, on_window)
            v.sem_inc(s_whole, 1)
            v.wait_ge(s_deg, 1)
            v.tensor_copy(c["deg"][:, :], ps_deg[0:P, 0:T])

        @block.tensor
        def _(pe):
            def on_window(n, m):
                pe.wait_ge(s_hot2, m + 1)
                products(pe, 0, low[:, 0, :, :], hot[:, 0, :, :]).then_inc(s_bank2, 1)

            def degrees_of(t):
                for k in range(T):
                    last = pe.matmul(ps_deg[:, bass.ds(t, 1)], at[:, k, bass.ds(t * P, 128)], ones[:, 0:1],
                                     start=(k == 0), stop=(k == T - 1))
                return last
            pe.wait_ge(s_one, 1)
            for t in range(T - 1):
                degrees_of(t)
            rounds_and_windows(pe, lambda r: None, on_window)
            n_tile = pe.value_load(further[0:1, 2:3], min_val=1, max_val=T - 1)
            pe.wait_ge(s_whole, 1)
            with pe.Fori(0, n_tile) as t:
                degrees_of(t)
            degrees_of(T - 1).then_inc(s_deg, 1)


def degrees(c):
    nc, sem, at, ident = c["nc"], c["sem"], c["at"], c["ident"]
    with ExitStack() as st:
        def sb(name, shape, dt):
            return st.enter_context(nc.sbuf_tensor(name, shape, dt))
        deg = c["deg"]
        tri, pidx, fidx = sb("tri", [P, P], F32), sb("d_pidx", [P, 1], F32), sb("d_fidx", [P, P], F32)
        one_row = sb("one_row", [1, P], F32)
        loops, y, e, root = (sb(f"d_{n}", [P, T], F32) for n in ("loops", "y", "e", "root"))
        ps2 = st.enter_context(nc.psum_tensor("end_ps", [128, BANK], F32))
        flat = at[:, :, :].rearrange("p t d -> p (t d)")

        def diagonals(eng, tiles):
            for k in tiles:
                a = flat[:, k * (ATW + P):k * (ATW + P) + P]
                eng.tensor_tensor(a, a, ident[0:P, 0:P], ALU.add)

        s_tri, s_sq, s_ch, s_end, s_iota, s_root = (sem(f"d_{n}") for n in ("tri", "sq", "chain", "end", "iota", "root"))
        with nc.Block() as block:
            @block.gpsimd
            def _(pool):
                pool.iota(pidx[:, :], pattern=[[0, 1]], base=0, channel_multiplier=1,
                          allow_small_or_imprecise_dtypes=True).then_inc(s_iota, 1)
                pool.iota(fidx[:, :], pattern=[[1, P]], base=0, channel_multiplier=0,
                          allow_small_or_imprecise_dtypes=True).then_inc(s_iota, 1)
                diagonals(pool, range(T // 2 + 3, T))

            @block.tensor
            def _(pe):
                pe.wait_ge(s_tri, 1)
                pe.matmul(ps2[0:P, 0:T], tri[:, :], deg[:, :], start=True, stop=False)
                pe.matmul(ps2[0:P, 0:T], one_row[:, :], c["start_f"][:, :], start=False, stop=True).then_inc(s_end, 1)

            @block.scalar
            def _(act):
                act.wait_ge(s_sq, 1)
                act.activation(root[:, :], loops[:, :], ACT.Sqrt).then_inc(s_root, 1)

            @block.vector
            def _(v):
                ch = Chain(v, s_ch)
                v.memset(one_row[:, :], 1.0)
                v.wait_ge(s_iota, 2)
                v.tensor_scalar(tri[:, :], fidx[:, :], pidx[:, :], None, ALU.is_ge).then_inc(s_tri, 1)
                v.tensor_scalar(c["has_in"][:, :], deg[:, :], 1.0, None, ALU.min)
                v.tensor_scalar(loops[:, :], deg[:, :], 1.0, None, ALU.add).then_inc(s_sq, 1)
                v.wait_ge(s_sq, 1)
                diagonals(v, range(0, T // 2 + 3))
                v.wait_ge(s_root, 1)
                ch(v.reciprocal(y[:, :], root[:, :]))
                ch(v.tensor_tensor(e[:, :], y[:, :], y[:, :], ALU.mult))
                ch(v.tensor_tensor(e[:, :], e[:, :], loops[:, :], ALU.mult))
                ch(v.tensor_scalar(e[:, :], e[:, :], -0.5, 1.5, ALU.mult, ALU.add))
                ch(v.tensor_tensor(c["dinv"][:, :], y[:, :], e[:, :], ALU.mult))
                v.tensor_scalar(c["dinv_lo"][:, :], c["dinv"][:, :], LO, None, ALU.mult)
                v.tensor_copy(c["ident16"][:, :], ident[0:P, 0:P])
                v.scalar_tensor_tensor(c["dsqrt"][:, :], loops[:, :], 1.0 / LO, c["dinv"][:, :], ALU.mult, ALU.mult)
                v.wait_ge(s_end, 1)
                ch(v.tensor_scalar(e[:, :], ps2[0:P, 0:T], 1.0, 0.0, ALU.subtract, ALU.max))
                v.tensor_copy(c["end_idx"][:, :], e[:, :])


def row_vector(c, name, n):
    return c["w"][name].rearrange("(o f) -> o f", o=1).to_broadcast([n, F])


def hop_state(c, st, tag):
    nc = c["nc"]

    def sb(name, shape, dt):
        return st.enter_context(nc.sbuf_tensor(f"{tag}_{name}", shape, dt))

    wide = sb("wide", [P, N], F32)
    return dict(u=[sb("u0", [P, T, 2 * F], F16), sb("u1", [P, T, 2 * F], F16)], uf=sb("uf", [P, T, F], F32),
                wide=wide, xa=wide[:, 0:T * F].rearrange("p (t f) -> p t f", f=F),
                clo=wide[:, T * F:(T + HB) * F].rearrange("p (b f) -> p b f", f=F),
                cf=sb("cf", [P, T], F32), cl=sb("cl", [P, T], F32))


class RowNorm:

    def __init__(self, c, st, tag, xs, sq, n=G):
        self.c, self.xs, self.n = c, xs, n
        nc = c["nc"]
        self.sq = sq
        self.mean, self.var, self.y, self.e = (
            st.enter_context(nc.sbuf_tensor(f"{tag}_{k}", [P, n], F32)) for k in ("mean", "var", "y", "e"))
        self.s_mid, self.s_sq, self.s_var, self.s_root = (c["sem"](f"{tag}_{k}") for k in ("mid", "sq", "var", "root"))
        self.groups = 0

    def vector(self, v, ch, g, h):
        x = self.xs[:, g * self.n:(g + 1) * self.n, :]
        sq = self.sq
        mean, var, y, e = (a[:, :] for a in (self.mean, self.var, self.y, self.e))
        ch(v.tensor_tensor(x, x, h, ALU.add))
        ch(v.reduce_sum(mean, x, X_AXIS))
        ch(v.tensor_scalar(mean, mean, 1.0 / F, None, ALU.mult))
        v.tensor_tensor(x, x, bc(mean, F), ALU.subtract).then_inc(self.s_mid, 1)
        v.wait_ge(self.s_sq, g + 1)
        ch(v.reduce_sum(var, sq, X_AXIS))
        v.tensor_scalar(var, var, 1.0 / F, EPS, ALU.mult, ALU.add).then_inc(self.s_var, 1)
        v.wait_ge(self.s_root, g + 1)
        ch(v.reciprocal(y, y))
        newton(v, ch, y, e, var)
        return v.tensor_tensor(x, x, bc(y, F), ALU.mult)

    def scalar(self, act, g):
        act.wait_ge(self.s_mid, g + 1)
        act.activation(self.sq, self.xs[:, g * self.n:(g + 1) * self.n, :], ACT.Square).then_inc(self.s_sq, 1)
        act.wait_ge(self.s_var, g + 1)
        act.activation(self.y[:, :], self.var[:, :], ACT.Sqrt).then_inc(self.s_root, 1)


def newton(v, ch, y, e, d):
    ch(v.tensor_tensor(e, y, y, ALU.mult))
    ch(v.tensor_tensor(e, e, d, ALU.mult))
    ch(v.tensor_scalar(e, e, -0.5, 1.5, ALU.mult, ALU.add))
    ch(v.tensor_tensor(y, y, e, ALU.mult))


def hops(c, tag, h, x0, keep, teleport, pairs, tail, norm=None, bias=None, out=None):
    nc, sem, at = c["nc"], c["sem"], c["at"]
    u, uf, xa, clo, cf, cl = (h[n] for n in ("u", "uf", "xa", "clo", "cf", "cl"))
    NG = T // G
    with ExitStack() as st:
        ps = st.enter_context(nc.psum_tensor(f"{tag}_ps", [128, HB, BANK], F32))
        s_ch, s_pre, s_prehi, s_cl, s_b = (sem(f"{tag}_{n}") for n in ("ch", "pre", "prehi", "cl", "b"))
        s_pe, s_clo, s_w, s_uf, s_hi, s_u = (sem(f"{tag}_{n}") for n in ("pe", "clo", "w", "uf", "hi", "u"))
        s_out, s_stored = sem(f"{tag}_out"), sem(f"{tag}_stored")
        rn = RowNorm(c, st, f"{tag}_n", norm, u[tail % 2][:, 0:G, :].bitcast(F32)) if norm is not None else None
        b_sb = st.enter_context(nc.sbuf_tensor(f"{tag}_bias", [P, F], F32)) if bias else None

        def program(eng, one):
            if pairs:
                with eng.Fori(0, pairs) as i:
                    for hop in range(2):
                        for t in range(T):
                            one(hop, t, i * (2 * T) + (hop * T + t + 1), False)
            for hop in range(tail):
                for t in range(T):
                    one(hop, t, (2 * pairs + hop) * T + t + 1, hop == tail - 1)

        with nc.Block() as block:
            @block.gpsimd
            def _(pool):
                pool.sem_inc(s_w, HB)

            @block.sync
            def _(sp):
                if bias:
                    sp.dma_start(b_sb[:, :], row_vector(c, bias, P)).then_inc(s_b, 16)
                if out is not None:
                    for g in range(NG):
                        sp.wait_ge(s_out, g + 1)
                        sp.dma_start(node_view(out)[:, g * G:(g + 1) * G, :], norm[:, g * G:(g + 1) * G, :]).then_inc(s_stored, 16)
                    sp.wait_ge(s_stored, 16 * NG)

            @block.tensor
            def _(pe):
                def one(hop, t, n, last_hop):
                    pe.wait_ge(s_w, n)
                    for k in range(T):
                        if t == 0:
                            pe.wait_ge(s_u, n + k)
                        last = pe.matmul(ps[:, t % HB, 0:2 * F], at[:, k, t * P:t * P + 128], u[hop][:, k, :],
                                         start=(k == 0), stop=(k == T - 1))
                    last.then_inc(s_pe, 1)
                program(pe, one)

            @block.scalar
            def _(act):
                for g in range(NG):
                    gs = slice(g * G, (g + 1) * G)
                    act.wait_ge(s_pre, g + 1)
                    act.activation(u[0][:, gs, 0:F], uf[:, gs, :], ACT.Copy, scale=1.0 / LO).then_inc(s_prehi, 1)
                act.activation(xa, uf[:, :, :], ACT.Copy, scale=teleport).then_inc(s_prehi, 1)
                act.wait_ge(s_cl, 1)

                def one(hop, t, n, last_hop):
                    b = t % HB
                    act.wait_ge(s_pe, n)
                    act.wait_ge(s_w, n)
                    act.activation(clo[:, b, :], ps[0:P, b, F:2 * F], ACT.Copy, scale=cl[:, t:t + 1]).then_inc(s_clo, 1)
                    if not last_hop:
                        act.wait_ge(s_uf, n)
                        act.activation(u[(hop + 1) % 2][:, t, 0:F], uf[:, t, :], ACT.Copy, scale=1.0 / LO).then_inc(s_hi, 1)
                    elif rn and t % G == G - 1:
                        rn.scalar(act, t // G)
                program(act, one)

            @block.vector
            def _(v):
                ch = Chain(v, s_ch)
                dinv = c["dinv"]
                for g in range(NG + 1):
                    if g < NG:
                        gs = slice(g * G, (g + 1) * G)
                        v.tensor_tensor(uf[:, gs, :], x0[:, gs, :], bc(c["dinv_lo"][:, gs], F), ALU.mult).then_inc(s_pre, 1)
                    if g:
                        gs = slice((g - 1) * G, g * G)
                        v.wait_ge(s_prehi, g)
                        v.scalar_tensor_tensor(u[0][:, gs, F:2 * F], u[0][:, gs, 0:F], -LO, uf[:, gs, :],
                                               ALU.mult, ALU.add).then_inc(s_u, G)
                ch(v.scalar_tensor_tensor(cf[:, :], dinv[:, :], LO * keep, dinv[:, :], ALU.mult, ALU.mult))
                v.tensor_scalar(cl[:, :], cf[:, :], 1.0 / LO, None, ALU.mult).then_inc(s_cl, 1)
                v.wait_ge(s_cl, 1)
                v.wait_ge(s_prehi, NG + 1)
                if bias:
                    v.wait_ge(s_b, 16)

                def finish(g):
                    gs = slice(g * G, (g + 1) * G)
                    ch(v.tensor_tensor(uf[:, gs, :], uf[:, gs, :], bc(c["dsqrt"][:, gs], F), ALU.mult))
                    if bias:
                        ch(v.tensor_tensor(uf[:, gs, :], uf[:, gs, :], b_sb[:, :].unsqueeze(1).to_broadcast([P, G, F]), ALU.add))
                    if rn:
                        rn.vector(v, ch, g, uf[:, gs, :]).then_inc(s_out, 1)

                def one(hop, t, n, last_hop):
                    b = t % HB
                    v.wait_ge(s_clo, n)
                    v.scalar_tensor_tensor(uf[:, t, :], ps[0:P, b, 0:F], cf[:, t:t + 1], clo[:, b, :],
                                           ALU.mult, ALU.add).then_inc(s_w, 1)
                    v.wait_ge(s_w, n + HB)
                    v.tensor_tensor(uf[:, t, :], uf[:, t, :], xa[:, t, :], ALU.add).then_inc(s_uf, 1)
                    if not last_hop:
                        v.wait_ge(s_hi, n)
                        v.scalar_tensor_tensor(u[(hop + 1) % 2][:, t, F:2 * F], u[(hop + 1) % 2][:, t, 0:F], -LO,
                                               uf[:, t, :], ALU.mult, ALU.add).then_inc(s_u, 1)
                    elif t % G == G - 1:
                        v.wait_ge(s_uf, n)
                        finish(t // G)
                program(v, one)


def node_product(c, tag, xs, w1, w2=None, bias=None, hs=None, graph_norm=False, y16=None, conv=None):
    nc, sem, ident = c["nc"], c["sem"], c["ident"]
    m = 2 * F if w2 else F
    per = 2 if w2 else G
    turns = [range(i, min(i + BLK, T)) for i in range(0, T, BLK)]
    batches = [range(i, min(i + per, T)) for i in range(0, T, per)]
    kk = F + 1 if w2 else F
    with ExitStack() as st:
        def sb(name, shape, dt=F32):
            return st.enter_context(nc.sbuf_tensor(f"{tag}_{name}", shape, dt))
        wc = sb("w", [kk, m])
        xt = sb("xt", [kk, N]) if w2 else hs["wide"][0:F, :]
        y = y16 if w2 else hs["uf"]
        root = conv.root if conv else sb("root", [P, T, F]) if w2 else None
        par = sb("par", [F, 3]) if graph_norm else None
        part = sb("part", [F, 2 * len(turns)]) if graph_norm else None
        col = sb("col", [F, 8]) if graph_norm else None
        junk = hs["u"][0] if graph_norm else None
        pt = st.enter_context(nc.psum_tensor(f"{tag}_pt", [128, 3, BANK], F32))
        py = st.enter_context(nc.psum_tensor(f"{tag}_py", [128, 4, BANK], F32))
        s_w, s_scaled, s_t, s_c, s_y, s_hi, s_o, s_st, s_ch, s_n, s_m = (
            sem(f"{tag}_{n}") for n in ("w", "scaled", "t", "c", "y", "hi", "o", "st", "ch", "n", "m"))
        n_w = 16 * (1 + 2 * bool(w2) + 3 * graph_norm)
        NT = len(turns)

        def of(r, width):
            b = r.start // per
            return py[0:P, b % 4, 0:len(r) * m].rearrange("p (t f) -> p t f", f=m)[:, :, width]

        def groups_before(b):
            return -(-min(T, (-(-batches[b].stop // BLK) + 1) * BLK) // G)

        with nc.Block() as block:
            @block.sync
            def _(sp):
                if conv:
                    conv.sync(sp)
                sp.dma_start(wc[0:F, 0:F], c["w"][w1]).then_inc(s_w, 16)
                if graph_norm:
                    with nc.allow_non_contiguous_dma(reason="vectors of F values, one to a partition"):
                        for i, name in enumerate(("gn_weight", "gn_bias", "gn_scale")):
                            sp.dma_start(par[:, i:i + 1], c["w"][name].rearrange("(f o) -> f o", o=1)).then_inc(s_w, 16)
                if w2:
                    sp.dma_start(wc[0:F, F:m], c["w"][w2]).then_inc(s_w, 16)
                    sp.dma_start(wc[F:kk, F:m], c["w"][bias].rearrange("(o f) -> o f", o=1)).then_inc(s_w, 16)
                    yv, rv = node_view(c["y_d"]), c["root_d"]
                    cuts = [0, 6, 12, 18, 22, T]
                    for a, b in zip(cuts, cuts[1:]):
                        sp.wait_ge(s_o, -(-b // per))
                        sp.dma_start(yv[:, a:b, :], y[:, a:b, :]).then_inc(s_st, 16)
                        sp.dma_start(rv[:, a:b, :], root[:, a:b, :]).then_inc(s_st, 16)
                    sp.wait_ge(s_st, 32 * (len(cuts) - 1))

            @block.tensor
            def _(pe):
                def turn(i):
                    if i >= 3:
                        pe.wait_ge(s_c, i - 2)
                    if conv:
                        pe.wait_ge(conv.s_ready, -(-turns[i].stop // G))
                    for t in turns[i]:
                        last = pe.transpose(pt[0:F, i % 3, (t % BLK) * P:(t % BLK + 1) * P], xs[:, t, :], ident[0:P, 0:P])
                    last.then_inc(s_t, 1)

                for i in range(NT if graph_norm else 2):
                    turn(i)
                pe.wait_ge(s_w, n_w)
                if w2:
                    pe.wait_ge(s_scaled, 3)
                if graph_norm:
                    pe.wait_ge(s_n, NT + 1)
                done = NT if graph_norm else 2
                for b, r in enumerate(batches):
                    while done < NT and r.stop > (done - 1) * BLK:
                        turn(done)
                        done += 1
                    if not graph_norm:
                        pe.wait_ge(s_c, (r.stop - 1) // BLK + 1)
                    if b >= 4:
                        pe.wait_ge(s_o, b - 3)
                    for j, t in enumerate(r):
                        last = pe.matmul(py[0:P, b % 4, j * m:(j + 1) * m], xt[:, t * P:(t + 1) * P], wc[:, :],
                                         start=True, stop=True)
                    last.then_inc(s_y, 1)

            @block.scalar
            def _(act):
                def copy(i):
                    r = turns[i]
                    act.wait_ge(s_t, i + 1)
                    a = dict(accum_out=part[:, i:i + 1]) if graph_norm else {}
                    act.activation(xt[0:F, r.start * P:r.stop * P], pt[0:F, i % 3, 0:len(r) * P], ACT.Copy, **a).then_inc(s_c, 1)

                if graph_norm:
                    for i in range(NT):
                        copy(i)
                    act.wait_ge(s_m, 1)
                    for i, r in enumerate(turns):
                        act.activation(junk[0:F, :, :].rearrange("p t f -> p (t f)")[:, r.start * P:r.stop * P],
                                       xt[0:F, r.start * P:r.stop * P], ACT.Square, bias=col[:, 0:1],
                                       accum_out=part[:, NT + i:NT + i + 1]).then_inc(s_n, 1)
                    act.wait_ge(s_m, 2)
                    act.activation(col[:, 2:3], col[:, 1:2], ACT.Sqrt).then_inc(s_m, 1)
                    act.wait_ge(s_m, 4)
                    act.activation(xt[0:F, :], xt[0:F, :], ACT.Relu, bias=col[:, 5:6], scale=col[:, 4:5]).then_inc(s_n, 1)
                elif not w2:
                    for i in range(NT):
                        copy(i)
                if w2:
                    done = 0
                    for b, r in enumerate(batches):
                        while done < NT and r.stop + 2 * per > done * BLK:
                            copy(done)
                            done += 1
                        act.wait_ge(s_y, b + 1)
                        act.activation(y[:, r.start:r.stop, 0:F], of(r, slice(0, F)), ACT.Copy).then_inc(s_hi, 1)

            @block.gpsimd
            def _(pool):
                if conv:
                    conv.gpsimd(pool)

            @block.vector
            def _(v):
                ch = Chain(v, s_ch)
                if w2:
                    v.memset(xt[F:kk, :], 1.0).then_inc(s_scaled, 1)
                    v.memset(wc[F:kk, 0:F], 0.0).then_inc(s_scaled, 1)
                    v.wait_ge(s_w, n_w)
                    v.tensor_scalar(wc[0:F, 0:F], wc[0:F, 0:F], YS, None, ALU.mult).then_inc(s_scaled, 1)
                if graph_norm:
                    v.wait_ge(s_w, n_w)
                    v.wait_ge(s_c, NT)
                    ch(v.reduce_sum(col[:, 1:2], part[:, 0:NT], X_AXIS))
                    v.scalar_tensor_tensor(col[:, 0:1], col[:, 1:2], -1.0 / N, par[:, 2:3], ALU.mult, ALU.mult).then_inc(s_m, 1)
                    v.wait_ge(s_m, 1)
                    v.wait_ge(s_n, NT)
                    ch(v.reduce_sum(col[:, 1:2], part[:, NT:2 * NT], X_AXIS))
                    ch(v.tensor_scalar(col[:, 1:2], col[:, 1:2], 1.0 / N, EPS, ALU.mult, ALU.add))
                    v.sem_inc(s_m, 1)
                    v.wait_ge(s_m, 3)
                    ch(v.reciprocal(col[:, 3:4], col[:, 2:3]))
                    newton(v, ch, col[:, 3:4], col[:, 6:7], col[:, 1:2])
                    ch(v.tensor_tensor(col[:, 4:5], col[:, 3:4], par[:, 0:1], ALU.mult))
                    v.scalar_tensor_tensor(col[:, 5:6], col[:, 0:1], col[:, 4:5], par[:, 1:2], ALU.mult, ALU.add).then_inc(s_m, 1)
                group = 0
                for b, r in enumerate(batches):
                    while conv and group < groups_before(b):
                        conv.vector(v, ch, group)
                        group += 1
                    if w2:
                        v.wait_ge(s_hi, b + 1)
                        v.tensor_tensor(y[:, r.start:r.stop, F:m], of(r, slice(0, F)), y[:, r.start:r.stop, 0:F], ALU.subtract)
                        v.tensor_copy(root[:, r.start:r.stop, :], of(r, slice(F, m))).then_inc(s_o, 1)
                    else:
                        v.wait_ge(s_y, b + 1)
                        v.tensor_copy(y[:, r.start:r.stop, :], of(r, slice(0, F))).then_inc(s_o, 1)


def edge_conv(c, tag, ea_t, w_edge, y):
    nc, ident, ident16 = c["nc"], c["ident"], c["ident16"]
    n_it = C // (G * G)
    HOT_G = G - 1
    HE = BLK * P
    OH = 5
    slot, ago = [q % 2 for q in range(G)], [1, 3] + [2] * (G - 2)
    slot3, ago3 = [0, 1, 2, 0, 1], [2, 2, 5, 3, 3]
    uses, nth = [2, 2, 1], [0, 0, 0, 1, 1]
    blocks = [range(0, 6), range(6, 12), range(12, 18), range(18, T)]
    with ExitStack() as st:
        sem = st.enter_context(phase_semaphores(nc))

        def sb(name, shape, dt):
            return st.enter_context(nc.sbuf_tensor(f"{tag}_{name}", shape, dt))
        gat = sb("gathered", [P, (G - 1) * G + 1, 2 * F], F16)
        idx_all, idx = c["idx_all"], sb("idx", [P, G, G], I32)
        comb = sb("scan_and_attr", [128, 3, GE], F32)
        mk = sb("mask", [F, 3, GE], BF16)
        back = sb("back", [P, 3, G * F], F32)
        we = sb("we", [128, F], F32)
        srcs = sb("srcs", [P, HE], F16)
        hot = sb("hot", [P, OH, HE], F16)
        nodes = sb("nodes", [P, T], F32)
        msg = st.enter_context(nc.psum_tensor(f"{tag}_msg", [128, 2, 2, BANK], F32))
        taken = st.enter_context(nc.psum_tensor(f"{tag}_taken", [128, BANK], F32))
        tr = st.enter_context(nc.psum_tensor(f"{tag}_tr", [128, 2, BANK], F32))
        s_w, s_init, s_idx, s_msg, s_scan, s_half, s_tr, s_back, s_gate, s_srcs, s_oh, s_took = (
            sem(f"{tag}_{n}") for n in
            ("w", "init", "idx", "msg", "scan", "half", "tr", "back", "gate", "srcs", "oh", "took"))
        s_gat = [sem(f"{tag}_gat{q}") for q in range(G)]
        s_ea, s_mk, s_st = ([sem(f"{tag}_{n}{k}") for k in range(3)] for n in ("ea", "mk", "st"))
        scan_v = c["scan_d"].rearrange("(g j p) f -> g p j f", j=G, p=P)

        def nth_use(i, q):
            return i * uses[slot3[q]] + nth[q]

        def gathered_by(q):
            return [G - 1] if q == HOT_G else range(G)

        def bank_a(q):
            return taken[0:F, :] if q == HOT_G else msg[0:F, slot[q], 0, :]

        with nc.Block() as block:
            @block.sync
            def _(sp):
                sp.dma_start(we[F:128, :], c["w"][w_edge]).then_inc(s_w, 16)
                with sp.Fori(0, n_it) as i:
                    sp.wait_ge(s_oh, i * T + 1)
                    sp.sem_inc(s_gate, 1)
                    sp.dma_start(srcs[:, :], c["src_d"][:, bass.ds(i * (G * GE) + HOT_G * GE, HE)].to_broadcast([P, HE])).then_inc(s_srcs, 16)
                    for q in range(G):
                        n = i * G + q
                        k = slot3[q]
                        sp.wait_ge(s_msg, n + (G + 1 - ago3[q]))
                        sp.sem_inc(s_gate, 1)
                        sp.dma_start(comb[F:128, k, :], ea_t[:, bass.ds(n * GE, GE)]).then_inc(s_ea[k], 16)
                        sp.wait_ge(s_scan, n + (G + 1 - ago3[q]))
                        sp.sem_inc(s_gate, 1)
                        sp.dma_start(mk[:, k, :], c["mask_d"][:, bass.ds(n * GE, GE)].to_broadcast([F, GE])).then_inc(s_mk[k], 16)

            @block.gpsimd
            def _(pool):
                for s in (s_msg, s_scan, s_tr, s_back):
                    pool.sem_inc(s, G)
                pool.sem_inc(s_oh, 1)
                pool.sem_inc(s_took, OH)
                for s in s_st:
                    pool.sem_inc(s, 16)
                pool.iota(nodes[:, :], pattern=[[P, T]], base=-SRC_MID, channel_multiplier=1,
                          allow_small_or_imprecise_dtypes=True).then_inc(s_init, 1)
                with pool.Fori(0, n_it) as i:
                    for q in range(G):
                        n = i * G + q
                        pool.wait_ge(s_msg, n + 1)
                        pool.wait_ge(s_idx, n + 1)
                        pool.sem_inc(s_gate, 1)
                        for j in gathered_by(q):
                            pool.indirect_dma_start(
                                out=gat[:, q * G + j if q < HOT_G else q * G, :], out_offset=None, in_=c["y_d"],
                                in_offset=bass.IndirectOffsetOnAxis(ap=idx[:, q, j:j + 1], axis=0),
                            ).then_inc(s_gat[q], 16)

            @block.tensor
            def _(pe):
                def messages(i, q):
                    n = i * G + q
                    k = slot3[q]
                    pe.wait_ge(s_scan, n + (G + 1 - ago[q]))
                    pe.wait_ge(s_ea[k], 16 * nth_use(i, q) + 16)
                    loads = len(gathered_by(q))
                    pe.wait_ge(s_gat[q], 16 * loads * i + 16 * loads)
                    pe.matmul(bank_a(q)[:, 0:HE], we[F:128, :], comb[F:128, k, 0:HE], start=(q != HOT_G), stop=(q == HOT_G))
                    pe.matmul(msg[0:F, slot[q], 1, 0:P], we[F:128, :], comb[F:128, k, HE:GE], start=True, stop=False)
                    for j in gathered_by(q):
                        to = msg[0:F, slot[q], 1, 0:P] if j == G - 1 else bank_a(q)[:, j * P:(j + 1) * P]
                        row = gat[:, q * G + j if q < HOT_G else q * G, :]
                        pe.matmul(to, row[:, 0:F], ident16[:, :], start=False, stop=False)
                        last = pe.matmul(to, row[:, F:2 * F], ident16[:, :], start=False, stop=(j >= BLK - 1))
                    last.then_inc(s_msg, 1)

                def take(i, tiles):
                    for t in tiles:
                        if t == 0:
                            pe.wait_ge(s_scan, i * G + G)
                        pe.wait_ge(s_oh, i * T + t + 2)
                        pe.matmul(taken[0:F, 0:HE], y[:, t, 0:F], hot[:, t % OH, :], start=(t == 0), stop=False)
                        pe.matmul(taken[0:F, 0:HE], y[:, t, F:2 * F], hot[:, t % OH, :], start=False, stop=False).then_inc(s_took, 1)

                def turn_back(i, q):
                    n = i * G + q
                    pe.wait_ge(s_back, n + (G + 1 - ago[q]))
                    pe.wait_ge(s_scan, n + (G + 1))
                    for j in range(G):
                        last = pe.transpose(tr[0:P, slot[q], j * F:(j + 1) * F], comb[0:F, slot3[q], j * P:(j + 1) * P],
                                            ident[0:F, 0:F])
                    last.then_inc(s_tr, 1)

                pe.wait_ge(s_w, 17)
                with pe.Fori(0, n_it) as i:
                    for q in range(G):
                        messages(i, q)
                        if q:
                            turn_back(i, q - 1)
                        if q < HOT_G:
                            take(i, blocks[q])
                    turn_back(i, G - 1)

            @block.vector
            def _(v):
                v.memset(comb[0:F, slot3[G - 1], GE - 1:GE], 0.0).then_inc(s_init, 1)
                for q in range(G):
                    v.tensor_copy(idx[:, q, :], idx_all[:, q * G:(q + 1) * G]).then_inc(s_idx, 1)
                v.wait_ge(s_init, 2)
                v.wait_ge(s_w, 16)
                v.tensor_scalar(we[F:128, :], we[F:128, :], YS, None, ALU.mult).then_inc(s_w, 1)

                def one_hots(i, tiles):
                    for t in tiles:
                        if t == 0:
                            v.wait_ge(s_srcs, 16 * i + 16)
                        v.wait_ge(s_took, i * T + t + 1)
                        v.tensor_scalar(hot[:, t % OH, :], srcs[:, :], nodes[:, t:t + 1], None, ALU.is_equal).then_inc(s_oh, 1)

                with v.Fori(0, n_it) as i:
                    for q in range(G):
                        n = i * G + q
                        k = slot3[q]
                        if q < HOT_G:
                            one_hots(i, blocks[q])
                        v.wait_ge(s_mk[k], 16 * nth_use(i, q) + 16)
                        v.wait_ge(s_tr, n + (G + 1 - ago3[q]))
                        v.wait_ge(s_scan, n + G)
                        v.wait_ge(s_msg, n + (G + 1))
                        v.tensor_tensor_scan(comb[0:F, k, 0:HE], mk[:, k, 0:HE], bank_a(q)[:, 0:HE],
                                             comb[0:F, slot3[(q - 1) % G], GE - 1:GE], ALU.add, ALU.max).then_inc(s_half, 1)
                        v.wait_ge(s_half, n + 1)
                        v.tensor_tensor_scan(comb[0:F, k, HE:GE], mk[:, k, HE:GE], msg[0:F, slot[q], 1, 0:P],
                                             comb[0:F, k, HE - 1:HE], ALU.add, ALU.max).then_inc(s_scan, 1)
                        v.tensor_copy(idx[:, q, :], idx_all[:, bass.ds((n + G) * G, G)]).then_inc(s_idx, 1)

            @block.scalar
            def _(act):
                with act.Fori(0, n_it) as i:
                    for q in range(G):
                        n = i * G + q
                        k = slot3[q]
                        act.wait_ge(s_st[k], 16 * nth_use(i, q) + 16)
                        act.wait_ge(s_tr, n + (G + 1))
                        act.activation(back[:, k, :], tr[0:P, slot[q], 0:G * F], ACT.Copy, scale=1.0 / YS).then_inc(s_back, 1)
                        act.wait_ge(s_back, n + (G + 1))
                        act.dma_start(scan_v[bass.ds(n, 1), :, :, :].rearrange("o p j f -> (o p) j f"),
                                      back[:, k, :].rearrange("p (j f) -> p j f", f=F)).then_inc(s_st[k], 16)
                for k in range(3):
                    act.wait_ge(s_st[k], 16 * uses[k] * n_it + 16)


class ConvResult:

    def __init__(self, c, st, tag, res):
        self.c, self.res = c, res
        self.root = st.enter_context(c["nc"].sbuf_tensor(f"{tag}_root", [P, T, F], F32))
        self.s_maxima = [c["sem"](f"{tag}_maxima{g}") for g in range(T // G)]
        self.s_root, self.s_ready = c["sem"](f"{tag}_root"), c["sem"](f"{tag}_ready")

    def gpsimd(self, pool):
        for t in range(T):
            pool.indirect_dma_start(out=self.res[:, t, :], out_offset=None, in_=self.c["scan_d"],
                                    in_offset=bass.IndirectOffsetOnAxis(ap=self.c["end_idx"][:, t:t + 1], axis=0),
                                    ).then_inc(self.s_maxima[t // G], 16)

    def sync(self, sp):
        sp.dma_start(self.root[:, :, :], self.c["root_d"]).then_inc(self.s_root, 16)

    def vector(self, v, ch, g):
        res, root = (a[:, g * G:(g + 1) * G, :] for a in (self.res, self.root))
        v.wait_ge(self.s_root, 16)
        v.wait_ge(self.s_maxima[g], 16 * G)
        ch(v.tensor_tensor(res, res, bc(self.c["has_in"][:, g * G:(g + 1) * G], F), ALU.mult))
        ch(v.tensor_tensor(root, root, res, ALU.add))
        ch(v.scalar_tensor_tensor(res, root, 0.01, root, ALU.mult, ALU.max))
        v.sem_inc(self.s_ready, 1)


def conv_result(c, tag, res, norm):
    nc, sem = c["nc"], c["sem"]
    with ExitStack() as st:
        conv = ConvResult(c, st, tag, res)
        s_ch = sem(f"{tag}_ch")
        sq = st.enter_context(nc.sbuf_tensor(f"{tag}_sq", [P, G, F], F32))
        rn = RowNorm(c, st, f"{tag}_n", norm, sq[:, :, :])
        with nc.Block() as block:
            @block.gpsimd
            def _(pool):
                conv.gpsimd(pool)

            @block.sync
            def _(sp):
                conv.sync(sp)

            @block.scalar
            def _(act):
                for g in range(T // G):
                    rn.scalar(act, g)

            @block.vector
            def _(v):
                ch = Chain(v, s_ch)
                for g in range(T // G):
                    conv.vector(v, ch, g)
                    rn.vector(v, ch, g, res[:, g * G:(g + 1) * G, :])


_WEIGHTS = {"W1_msg": "L1_gnn_W1_msg", "W1_edge": "L1_gnn_W1_edge", "W1_root": "L1_gnn_W1_root", "b1": "L1_gnn_b1",
            "W2_msg": "L1_gnn_W2_msg", "W2_edge": "L1_gnn_W2_edge", "W2_root": "L1_gnn_W2_root", "b2": "L1_gnn_b2",
            "g_W1": "L3_gnn_W1", "g_b1": "L3_gnn_b1", "gn_weight": "L3_gnn_gn_weight", "gn_bias": "L3_gnn_gn_bias",
            "gn_scale": "L3_gnn_gn_mean_scale", "g_W2": "L3_gnn_W2", "g_b2": "L3_gnn_b2"}


def kernel(**inputs):
    import numpy as np
    import concourse.bacc as bacc
    from concourse.bass_utils import run_bass_kernel_spmd

    nc = bacc.Bacc("TRN2", target_bir_lowering=False, num_devices=1)
    src = np.asarray(inputs["src"])
    arrays = {
        "x": np.ascontiguousarray(inputs["x"]),
        "src": np.ascontiguousarray(src),
        "dst": np.ascontiguousarray(inputs["dst"]),
        "src_cols": np.ascontiguousarray(src.reshape(C, P).T),
        "ea_t": np.ascontiguousarray(np.asarray(inputs["edge_attr_32"]).T),
    }
    for short, name in _WEIGHTS.items():
        arrays["w_" + short] = np.ascontiguousarray(inputs[name])
    aps = {n: nc.dram_tensor("in_" + n, a.shape, mybir.dt.from_np(a.dtype), kind="ExternalInput").ap()
           for n, a in arrays.items()}
    out = nc.dram_tensor("out_x", (N, F), F32, kind="ExternalOutput").ap()
    build(nc, aps["x"], aps["src"], aps["dst"], aps["src_cols"], aps["ea_t"], {n: aps["w_" + n] for n in _WEIGHTS}, out)
    r = run_bass_kernel_spmd(nc, [{"in_" + n: a for n, a in arrays.items()}], core_ids=[0])
    return r.results[0]["out_x"]
```
